# Optimizing a Trainium2 kernel written in Bass

```python
import numpy as np
import jax
import jax.numpy as jnp

def _softmax(x, axis=-1):
    return jax.nn.softmax(x, axis=axis)

def _gelu(x):
    return jax.nn.gelu(x, approximate=True)

def _silu(x):
    return jax.nn.silu(x)

def _sigmoid(x):
    return jax.nn.sigmoid(x)

def _layernorm(x, axis=-1, eps=1e-05):
    m = jnp.mean(x, axis=axis, keepdims=True)
    v = jnp.var(x, axis=axis, keepdims=True)
    return (x - m) / jnp.sqrt(v + eps)

def _scatter_add(tgt, idx, src, axis=0):
    return tgt.at[idx].add(src)

def _segment_sum(src, seg, n):
    return jax.ops.segment_sum(src, seg, n)
kernel_name = 'mk_gnn_preln_d1_gnn_r8_1a0c58'

def setup_inputs(seed: int=0):
    np.random.seed(seed)
    _w = jnp.asarray

    def _rec_inputs():
        import jax
        import jax.numpy as jnp
        _gk = jax.random.key(seed)
        x = -0.0003713 + 1 * jax.random.normal(jax.random.fold_in(_gk, 1), (12500, 128), jnp.float32)
        _s = jax.random.randint(jax.random.fold_in(_gk, 2), (100000,), 0, 12500, jnp.int32)
        _d = jax.random.randint(jax.random.fold_in(_gk, 3), (100000,), 0, 12500, jnp.int32)
        _loop = jnp.arange(12500, dtype=jnp.int32)
        src = jnp.concatenate([_s, _d, _loop])
        dst = jnp.concatenate([_d, _s, _loop])
        _o = jnp.argsort(dst, stable=True)
        src = src[_o]
        dst = dst[_o]
        return (x, src, dst)
    x, src, dst = _rec_inputs()

    def _L0_gnn_setup():
        import jax, jax.numpy as jnp
        import numpy as np
        N_NODES = 12500
        N_EDGES = 75000
        H = 128
        NUM_STEPS = 5
        key = jax.random.key(seed)
        ks = jax.random.split(key, 8)
        s = 0.05
        return {'x': jax.random.normal(ks[0], (N_NODES, H), dtype=jnp.float32), 'edge_index': jax.random.randint(ks[1], (2, N_EDGES), 0, N_NODES, dtype=jnp.int64), 'W_msg': jax.random.normal(ks[2], (H, H), dtype=jnp.float32) * s, 'b_msg': jax.random.normal(ks[3], (H,), dtype=jnp.float32) * s, 'W_ih': jax.random.normal(ks[4], (3 * H, H), dtype=jnp.float32) * s, 'W_hh': jax.random.normal(ks[5], (3 * H, H), dtype=jnp.float32) * s, 'b_ih': jax.random.normal(ks[6], (3 * H,), dtype=jnp.float32) * s, 'b_hh': jax.random.normal(ks[7], (3 * H,), dtype=jnp.float32) * s}
    _L0_gnn_all = _L0_gnn_setup()
    _L0_gnn_in = {k: v for k, v in _L0_gnn_all.items() if k in ('W_msg', 'b_msg', 'W_ih', 'W_hh', 'b_ih', 'b_hh')}
    del _L0_gnn_all
    return {'x': x, 'src': src, 'dst': dst, 'L0_gnn_W_msg': _L0_gnn_in['W_msg'], 'L0_gnn_b_msg': _L0_gnn_in['b_msg'], 'L0_gnn_W_ih': _L0_gnn_in['W_ih'], 'L0_gnn_W_hh': _L0_gnn_in['W_hh'], 'L0_gnn_b_ih': _L0_gnn_in['b_ih'], 'L0_gnn_b_hh': _L0_gnn_in['b_hh']}

def reference(x, src, dst, L0_gnn_W_msg, L0_gnn_b_msg, L0_gnn_W_ih, L0_gnn_W_hh, L0_gnn_b_ih, L0_gnn_b_hh):
    import jax
    import jax.numpy as jnp

    def _L0_gnn_ref(x, edge_index, W_msg, b_msg, W_ih, W_hh, b_ih, b_hh):
        import jax, jax.numpy as jnp
        import numpy as np
        N_NODES = 12500
        N_EDGES = 75000
        H = 128
        NUM_STEPS = 5
        num_nodes = x.shape[0]
        row, col = (edge_index[0], edge_index[1])

        def step(h, _):
            messages = h[col] @ W_msg.T + b_msg
            agg = jax.ops.segment_sum(messages, row, num_segments=num_nodes)
            gi = agg @ W_ih.T + b_ih
            gh = h @ W_hh.T + b_hh
            i_r, i_z, i_n = jnp.split(gi, 3, axis=-1)
            h_r, h_z, h_n = jnp.split(gh, 3, axis=-1)
            r = jax.nn.sigmoid(i_r + h_r)
            z = jax.nn.sigmoid(i_z + h_z)
            n = jnp.tanh(i_n + r * h_n)
            h_new = (1.0 - z) * n + z * h
            return (h_new, None)
        h, _ = jax.lax.scan(step, x, None, length=NUM_STEPS)
        return h
    edge_index = jnp.stack([src, dst])
    h = jnp.maximum(_layernorm(x, axis=-1), 0.0)
    x = x + _L0_gnn_ref(h, edge_index, L0_gnn_W_msg, L0_gnn_b_msg, L0_gnn_W_ih, L0_gnn_W_hh, L0_gnn_b_ih, L0_gnn_b_hh)
    return x

_drawn_inputs = setup_inputs


def setup_inputs(seed=0):
    import zlib

    import numpy as np

    out = dict(_drawn_inputs(seed))
    spreads = {}
    factors = {}
    for name, (base, spread) in spreads.items():
        noise = np.random.default_rng([zlib.crc32(name.encode()), seed]).standard_normal(out[name].shape)
        drawn = base * np.exp(spread * noise) if base else spread * noise
        out[name] = jnp.asarray(drawn.astype(out[name].dtype))
    for name, factor in factors.items():
        out[name] = (out[name] * factor).astype(out[name].dtype)
    return out
```

```python
from contextlib import ExitStack

import concourse.bass as bass
from concourse import mybir

ALU = mybir.AluOpType
ACT = mybir.ActivationFunctionType
AX_X = mybir.AxisListType.X
F32 = mybir.dt.float32
F16 = mybir.dt.float16
BF16 = mybir.dt.bfloat16
I32 = mybir.dt.int32
U16 = mybir.dt.uint16

P = 128
STEPS = 5
CHUNK = 512
GROUP = 4
ISETS = 4
PRIME = ISETS // 2
OHR = 4 * GROUP
SCALE = 2048.0
EPS = 1e-5
SC_HALF = 8
NO_NODE = 1023


def build_gnn(nc, x, src, dst, W_msg, b_msg, W_ih, W_hh, b_ih, b_hh, out):
    N, H = x.shape
    E = src.shape[0]
    assert H == P
    NCH = -(-N // CHUNK)
    NPAD = NCH * CHUNK
    NT = -(-N // P)
    K = -(-E // (P * 2 * SC_HALF)) * 2 * SC_HALF
    FULL = E // K
    REM = E - FULL * K
    assert FULL == P - 1
    GE = GROUP * P
    GMAX = -(-((P * K) // GE + NCH) // ISETS) * ISETS
    T = GMAX * GROUP
    LNT = 14
    assert NT % LNT == 0
    NLN = NT // LNT
    NFULL = N // P
    NREM = N - NFULL * P

    rec_dram = nc.dram_tensor("rec_dram", (P * T, 1), I32, kind="Internal").ap()
    hrows = nc.dram_tensor("hrows", (2 * NPAD, 2 * H), F16, kind="Internal").ap()

    with ExitStack() as ctx:
        def sb(name, shape, dt):
            return ctx.enter_context(nc.sbuf_tensor(name, shape, dt))

        def psum(name, shape, dt):
            return ctx.enter_context(nc.psum_tensor(name, shape, dt))

        def sem(name):
            return ctx.enter_context(nc.semaphore(name))

        ps_agg = psum("ps_agg", [P, 2 * CHUNK], F32)
        ps_r = psum("ps_r", [P, CHUNK], F32)
        ps_z = psum("ps_z", [P, CHUNK], F32)
        ps_in = psum("ps_in", [P, CHUNK], F32)
        ps_hn = psum("ps_hn", [P, CHUNK], F32)
        ps_rows = psum("ps_rows", [P, 8 * P], F16)
        ps_deg = psum("ps_deg", [P, CHUNK], F32)

        early = sb("early", [P, 4 * K], I32)
        src_sb = early[:, 0:K]
        dst_sb = early[:, K:2 * K]
        chunk_i = early[:, 2 * K:3 * K]
        scan = early[:, 3 * K:4 * K].bitcast(F32)
        idx_tab = early[:, 0:2 * T]
        loc_tab = early[:, 2 * T:3 * T].bitcast(F32)
        mid = sb("mid", [P, 3 * K], I32)
        pos = mid[:, 0:K].bitcast(F32)
        pos_i = mid[:, K:2 * K]
        rec = mid[:, 2 * K:3 * K]
        pos_hi = chunk_i
        chunk_b = sb("chunk_b", [P, K], BF16)
        mask = sb("mask", [P, K], U16)
        rec_sb = sb("rec_sb", [P, T], I32)
        fill = rec_sb
        sc_pos = sb("sc_pos", [P, 2 * SC_HALF], I32)
        sc_rec = sb("sc_rec", [P, 2 * SC_HALF], I32)

        iota_i = sb("iota_i", [P, CHUNK], I32)
        iota_h = sb("iota_h", [P, CHUNK], F16)
        iota_f = sb("iota_f", [P, P], F32)
        part_i = sb("part_i", [P, 1], I32)
        part_f = sb("part_f", [P, 1], F32)
        ident = sb("ident", [P, P], F32)
        ident_h = sb("ident_h", [P, P], F16)
        before = sb("before", [P, P], F32)
        ones_f = sb("ones_f", [P, P], F32)
        ones_h = sb("ones_h", [P, 1], F16)
        zeros_h = sb("zeros_h", [1, CHUNK], F16)
        cnt = sb("cnt", [P, NCH], F32)
        base = sb("base", [P, NCH], F32)
        grp_i = sb("grp_i", [P, NCH], I32)
        grp_f = sb("grp_f", [P, NCH], F32)
        cum = sb("cum", [P, 2, NCH], F32)
        start_f = sb("start_f", [P, NCH], F32)
        chunk_end = sb("chunk_end", [P, NCH + 1], I32)

        wmsg_sb = sb("wmsg_sb", [P, P], F32)
        wih_sb = sb("wih_sb", [P, 3, P], F32)
        whh_sb = sb("whh_sb", [P, 3, P], F32)
        wihT = sb("wihT", [P, 3 * P], F32)
        whhT = sb("whhT", [P, 3 * P], F32)
        wfT = sb("wfT", [P, 3 * P], F32)
        cdeg = sb("cdeg", [1, 3 * P], F32)
        bmsg_sb = sb("bmsg_sb", [P, 1], F32)
        bih_sb = sb("bih_sb", [P, 3], F32)
        bhh_sb = sb("bhh_sb", [P, 3], F32)
        bsum = sb("bsum", [P, 3], F32)

        hT = sb("hT", [P, NPAD], F32)
        deg = sb("deg", [1, NPAD], F32)
        xg = sb("xg", [P, 2, LNT, P], F32)
        stats = sb("stats", [P, 6], F32)
        mv = sb("mv", [P, LNT, 2], F32)
        std = sb("std", [P, LNT], F32)
        rstd = sb("rstd", [P, LNT], F32)
        lnrow = sb("lnrow", [P, LNT, 2, P], F16)

        idx_slot = sb("idx_slot", [P, ISETS * GROUP], I32)
        G = sb("G", [P, 2 * GROUP * 2 * H], F16)
        OH = mid[:, 0:OHR * CHUNK // 2].bitcast(F16)
        srz = lnrow[:].rearrange("p t a k -> p (t a k)").bitcast(F32)
        S = srz[:, 0:CHUNK]
        r_sb = srz[:, CHUNK:2 * CHUNK]
        z_sb = srz[:, 2 * CHUNK:3 * CHUNK]
        t_sb = sb("t_sb", [P, CHUNK], F32)
        n_sb = sb("n_sb", [P, CHUNK], F32)
        hi = sb("hi", [P, CHUNK], F16)
        lo = sb("lo", [P, CHUNK], F16)
        rowbuf = iota_i[:].bitcast(F16)

        edges_padded = sem("edges_padded")
        edges_loaded = sem("edges_loaded")
        fill_ready = sem("fill_ready")
        zeros_ready = sem("zeros_ready")
        zeros_stored = sem("zeros_stored")
        rec_filled = sem("rec_filled")
        weights_loaded = sem("weights_loaded")
        iota_done = sem("iota_done")
        consts_ready = sem("consts_ready")
        dve_step = sem("dve_step")
        counts_ready = sem("counts_ready")
        prefix_ready = sem("prefix_ready")
        mask_step = sem("mask_step")
        rank_step = sem("rank_step")
        chunk_masked = sem("chunk_masked")
        chunk_ranked = sem("chunk_ranked")
        chunk_placed = sem("chunk_placed")
        pos_cleared = sem("pos_cleared")
        pos_ready = sem("pos_ready")
        slots_filled = [sem("slots_filled_0"), sem("slots_filled_1")]
        scattered = [sem("scattered_0"), sem("scattered_1")]
        rec_loaded = sem("rec_loaded")
        tables_ready = sem("tables_ready")
        x_loaded = [sem("x_loaded_0"), sem("x_loaded_1")]
        var_ready = sem("var_ready")
        std_ready = sem("std_ready")
        ln_step = sem("ln_step")
        lnT_ready = sem("lnT_ready")
        lnT_copied = sem("lnT_copied")
        ln_rows_ready = sem("ln_rows_ready")
        w_turned = sem("w_turned")
        w_copied = sem("w_copied")
        idx_loaded = [sem(f"idx_loaded_{i}") for i in range(ISETS)]
        pool_turns = sem("pool_turns")
        gathered = [[sem(f"gathered_{a}_{j}") for j in range(GROUP)] for a in range(2)]
        oh_ready = sem("oh_ready")
        groups_done = sem("groups_done")
        agg_done = sem("agg_done")
        s_ready = sem("s_ready")
        gates_done = sem("gates_done")
        rz_ready = sem("rz_ready")
        t_done = sem("t_done")
        t2_ready = sem("t2_ready")
        n_ready = sem("n_ready")
        upd_step = sem("upd_step")
        h_ready = sem("h_ready")
        rows_turned = sem("rows_turned")
        rows_copied = sem("rows_copied")
        rows_stored = sem("rows_stored")
        fin_rows = [sem("fin_rows_0"), sem("fin_rows_1")]
        fin_step = sem("fin_step")
        fin_ready = sem("fin_ready")
        out_stored = sem("out_stored")

        block = ctx.enter_context(nc.Block())

        def x_tiles(t, g, first):
            lo_row = g * LNT * P
            n_full = min(LNT, NFULL - g * LNT)
            pieces = [(t[lo_row:lo_row + n_full * P, :].rearrange("(t p) f -> p t f", p=P), first[:, 0:n_full, :])]
            if n_full < LNT:
                pieces.append((t[NFULL * P:N, :], first[0:NREM, n_full, :]))
            return pieces

        def fin_bufs(b):
            return early[:, b * LNT * P:(b + 1) * LNT * P].bitcast(F16).rearrange("p (t k) -> p t k", k=2 * H)

        PIECES = [len(x_tiles(x, g, xg[:, 0])) for g in range(NLN)]

        def store_ln(sp, g):
            sp.wait_ge(ln_rows_ready, g + 1)
            at = g * LNT * P
            sp.dma_start(hrows[at:at + LNT * P, :].rearrange("(t p) k -> p t k", p=P),
                         lnrow[:].rearrange("p t a k -> p t (a k)")).then_inc(rows_stored, 16)

        def store_out(sp, g):
            sp.wait_ge(fin_ready, g + 1)
            for rows, tile in x_tiles(out, g, xg[:, g % 2]):
                sp.dma_start(rows, tile).then_inc(out_stored, 16)

        @block.sync
        def _(sp):
            sp.wait_ge(edges_padded, 2)
            for flat, tile in ((src, src_sb), (dst, dst_sb)):
                sp.dma_start(tile[0:FULL, :], flat[0:FULL * K].rearrange("(p k) -> p k", k=K)).then_inc(edges_loaded, 16)
                sp.dma_start(tile[FULL:P, 0:REM], flat[FULL * K:E].rearrange("(a k) -> a k", a=1)).then_inc(edges_loaded, 16)
            sp.wait_ge(fill_ready, 1)
            sp.dma_start(rec_dram.rearrange("(p t) o -> p (t o)", p=P), fill[:]).then_inc(rec_filled, 16)
            sp.wait_ge(zeros_ready, 1)
            zeros = hT[:].bitcast(F16)
            sp.dma_start(hrows[NPAD:2 * NPAD, :].rearrange("(p r) k -> p (r k)", p=P), zeros).then_inc(zeros_stored, 16)
            sp.dma_start(hrows[NT * P:NPAD, :].rearrange("(p r) k -> p (r k)", p=P),
                         zeros[:, 0:(NPAD - NT * P) // P * 2 * H]).then_inc(zeros_stored, 16)
            sp.dma_start(wmsg_sb[:], W_msg).then_inc(weights_loaded, 16)
            sp.dma_start(wih_sb[:], W_ih.rearrange("(g p) k -> p g k", p=P)).then_inc(weights_loaded, 16)
            sp.dma_start(whh_sb[:], W_hh.rearrange("(g p) k -> p g k", p=P)).then_inc(weights_loaded, 16)
            sp.dma_start(bmsg_sb[:], b_msg.rearrange("(p o) -> p o", o=1)).then_inc(weights_loaded, 16)
            for g in range(3):
                sp.dma_start(bih_sb[:, g:g + 1], b_ih[g * P:(g + 1) * P].rearrange("(p o) -> p o", o=1)).then_inc(weights_loaded, 16)
                sp.dma_start(bhh_sb[:, g:g + 1], b_hh[g * P:(g + 1) * P].rearrange("(p o) -> p o", o=1)).then_inc(weights_loaded, 16)
            for g in range(NLN):
                if g >= 2:
                    sp.wait_ge(ln_rows_ready, g - 1)
                    sp.wait_ge(lnT_copied, (g - 1) * LNT)
                for rows, tile in x_tiles(x, g, xg[:, g % 2]):
                    sp.dma_start(tile, rows).then_inc(x_loaded[g % 2], 16)
                if g >= 1:
                    store_ln(sp, g - 1)
            store_ln(sp, NLN - 1)
            for h in range(2):
                sp.wait_ge(scattered[h], 16 * SC_HALF * (K // (2 * SC_HALF)))
            sp.dma_start(rec_sb[:], rec_dram.rearrange("(p t) o -> p (t o)", p=P)).then_inc(rec_loaded, 16)
            sp.wait_ge(tables_ready, 1)
            total = sp.value_load(chunk_end[0:1, NCH:NCH + 1], min_val=1, max_val=GMAX)
            with sp.Fori(0, STEPS) as s:
                with sp.Fori(0, total, ISETS) as g:
                    for i in range(ISETS):
                        n = s * total + g + i + 1
                        for j in range(GROUP):
                            sp.wait_ge(gathered[i % 2][j], ((n + 1 - i % 2) // 2) * 16)
                        sp.dma_start(idx_slot[:, i * GROUP:(i + 1) * GROUP],
                                     idx_tab[:, bass.ds((s % 2) * T + (g + i).with_bounds(max_val=GMAX - 1) * GROUP, GROUP)]
                                     ).then_inc(idx_loaded[i], 16)
            sp.wait_ge(rows_stored, 16 * (NLN + STEPS * NCH))
            par = STEPS % 2
            for g in range(NLN):
                if g >= 2:
                    sp.wait_ge(fin_ready, g - 1)
                    sp.wait_ge(out_stored, 16 * sum(PIECES[:g - 1]))
                at = par * NPAD + g * LNT * P
                sp.dma_start(fin_bufs(g % 2), hrows[at:at + LNT * P, :].rearrange("(t p) k -> p t k", p=P)).then_inc(fin_rows[g % 2], 16)
                for rows, tile in x_tiles(x, g, xg[:, g % 2]):
                    sp.dma_start(tile, rows).then_inc(fin_rows[g % 2], 16)
                if g >= 1:
                    store_out(sp, g - 1)
            store_out(sp, NLN - 1)
            sp.wait_ge(out_stored, 16 * sum(PIECES))

        @block.gpsimd
        def _(pool):
            nc.gpsimd.iota(iota_i[:], pattern=[[1, CHUNK]], base=0, channel_multiplier=0).then_inc(iota_done, 1)
            nc.gpsimd.iota(part_i[:], pattern=[[0, 1]], base=0, channel_multiplier=1).then_inc(iota_done, 1)
            pool.wait_ge(iota_done, 2)
            for turn in range(PRIME):
                for k in range(2 * GROUP):
                    if turn:
                        pool.wait_ge(gathered[k // GROUP][k % GROUP], 16 * turn)
                    nc.gpsimd.indirect_dma_start(G[:, k * 2 * H:(k + 1) * 2 * H].bitcast(F32), None, x,
                                                 bass.IndirectOffsetOnAxis(ap=part_i[:, 0:1], axis=0)
                                                 ).then_inc(gathered[k // GROUP][k % GROUP], 16)
            pool.wait_ge(rec_filled, 16)
            with pool.Fori(1, K // (2 * SC_HALF) + 1) as i:
                for h in range(2):
                    pool.wait_ge(slots_filled[h], i)
                    pool.sem_inc(pool_turns, 1)
                    for j in range(h * SC_HALF, (h + 1) * SC_HALF):
                        nc.gpsimd.indirect_dma_start(
                            rec_dram, bass.IndirectOffsetOnAxis(ap=sc_pos[:, j:j + 1], axis=0),
                            sc_rec[:, j:j + 1], None).then_inc(scattered[h], 16)
            pool.wait_ge(rows_stored, 16 * NLN)
            pool.wait_ge(zeros_stored, 32)
            pool.wait_ge(tables_ready, 1)
            total = pool.value_load(chunk_end[0:1, NCH:NCH + 1], min_val=1, max_val=GMAX)
            with pool.Fori(0, STEPS) as s:
                pool.wait_ge(rows_stored, s * (16 * NCH) + 16 * NLN)
                first = pool.snap(s * total * 8)
                with pool.Fori(first + 8 * ISETS, first + total * 8 + 8 * ISETS, 8 * ISETS) as v:
                    for i in range(ISETS):
                        pool.wait_ge(groups_done, (v // 8) + i)
                        pool.wait_ge(idx_loaded[i], v // 2)
                        pool.sem_inc(pool_turns, 1)
                        for j in range(GROUP):
                            k, m = (i % 2) * GROUP + j, i * GROUP + j
                            nc.gpsimd.indirect_dma_start(
                                G[:, k * 2 * H:(k + 1) * 2 * H], None, hrows,
                                bass.IndirectOffsetOnAxis(ap=idx_slot[:, m:m + 1], axis=0)).then_inc(gathered[i % 2][j], 16)

        @block.scalar
        def _(act):
            def fill_half(i, h, wait):
                if wait is not None:
                    act.wait_ge(scattered[h], wait)
                col = i * (2 * SC_HALF) + h * SC_HALF
                lo_c, hi_c = h * SC_HALF, (h + 1) * SC_HALF
                nc.scalar.copy(sc_pos[:, lo_c:hi_c], pos_i[:, bass.ds(col, SC_HALF)])
                nc.scalar.copy(sc_rec[:, lo_c:hi_c], rec[:, bass.ds(col, SC_HALF)]).then_inc(slots_filled[h], 1)

            TURNS = K // (2 * SC_HALF)
            act.wait_ge(pos_ready, 1)
            for h in range(2):
                fill_half(0, h, None)
            cuts = [1] + [TURNS * (g + 1) // (NLN + 2) for g in range(NLN)] + [TURNS]
            for n in range(NLN + 1):
                with act.Fori(cuts[n], cuts[n + 1]) as i:
                    for h in range(2):
                        fill_half(i, h, i * (16 * SC_HALF))
                if n < NLN:
                    act.wait_ge(var_ready, n + 1)
                    nc.scalar.activation(std[:], mv[:, :, 1], ACT.Sqrt).then_inc(std_ready, 1)

            def scale_sum(q, first):
                act.wait_ge(agg_done, q)
                if first is not None:
                    nc.scalar.copy(deg[0:1, bass.ds(first, CHUNK)], ps_deg[0:1, :])
                nc.scalar.mul(S, ps_agg[:, bass.ds((q % 2) * CHUNK, CHUNK)], 1.0 / SCALE).then_inc(s_ready, 1)

            def gates(q):
                act.wait_ge(gates_done, q)
                act.wait_ge(h_ready, q)
                nc.scalar.activation(r_sb, ps_r[:], ACT.Sigmoid, bias=bsum[:, 0:1])
                nc.scalar.activation(z_sb, ps_z[:], ACT.Sigmoid, bias=bsum[:, 1:2]).then_inc(rz_ready, 1)

            def new(q):
                act.wait_ge(t2_ready, q)
                nc.scalar.activation(n_sb[:], t_sb[:], ACT.Tanh, bias=bih_sb[:, 2:3]).then_inc(n_ready, 1)

            def rows(q, s, c):
                act.wait_ge(rows_turned, q + 1)
                act.wait_ge(rows_stored, q * 16 + (16 * NLN - 16))
                nc.scalar.copy(rowbuf, ps_rows[:]).then_inc(rows_copied, 1)
                act.wait_ge(rows_copied, q + 1)
                at = ((s + 1) % 2) * NPAD + c * CHUNK
                act.dma_start(hrows[bass.ds(at, CHUNK), :].rearrange("(b p) k -> p b k", p=P),
                              rowbuf.rearrange("p (b k) -> p b k", k=2 * H)).then_inc(rows_stored, 16)

            act.sem_inc(rows_copied, 1)

            def step(s, first):
                q0 = s * NCH + 1
                scale_sum(q0, 0 if first else None)
                gates(q0)
                with act.Fori(1, NCH) as c:
                    q = s * NCH + c + 1
                    new(q - 1)
                    scale_sum(q, c * CHUNK if first else None)
                    gates(q)
                    rows(q - 1, s, c - 1)
                new(s * NCH + NCH)
                rows(s * NCH + NCH, s, NCH - 1)

            step(0, True)
            with act.Fori(1, STEPS) as s:
                step(s, False)

        @block.tensor
        def _(pe):
            pe.sem_inc(groups_done, 5)
            pe.sem_inc(rows_turned, 1)
            pe.wait_ge(counts_ready, 1)
            pe.matmul(ps_r[:, 0:NCH], lhsT=ones_f[:], rhs=cnt[:], start=True, stop=True)
            pe.matmul(ps_z[:, 0:NCH], lhsT=before[:], rhs=cnt[:], start=True, stop=True).then_inc(prefix_ready, 1)
            pe.wait_ge(weights_loaded, 16 * 10)
            for g in range(3):
                pe.transpose(ps_in[:, g * P:(g + 1) * P], wih_sb[:, g, :], ident[:])
            for g in range(3):
                mm = pe.transpose(ps_hn[:, g * P:(g + 1) * P], whh_sb[:, g, :], ident[:])
            mm.then_inc(w_turned, 1)
            pe.wait_ge(w_copied, 1)
            pe.matmul(ps_in[:, 0:3 * P], lhsT=wmsg_sb[:], rhs=wihT[:], start=True, stop=True)
            pe.matmul(ps_hn[0:1, 0:3 * P], lhsT=bmsg_sb[:, 0:1], rhs=wihT[:], start=True, stop=True).then_inc(w_turned, 1)
            for g in range(NLN):
                pe.wait_ge(ln_rows_ready, g + 1)
                for t in range(LNT):
                    n = g * LNT + t
                    if n >= 2:
                        pe.wait_ge(lnT_copied, n - 1)
                    bank = ps_agg[:, (n % 2) * CHUNK:(n % 2) * CHUNK + P]
                    pe.transpose(bank, xg[:, g % 2, t, :], ident[:]).then_inc(lnT_ready, 1)
            pe.wait_ge(w_copied, 3)
            pe.wait_ge(lnT_copied, NT)
            pe.wait_ge(tables_ready, 1)

            def sums(q, n0, c, first):
                start = pe.value_load(chunk_end[0:1, bass.ds(c, 1)], min_val=0, max_val=GMAX)
                end = pe.value_load(chunk_end[0:1, bass.ds(c + 1, 1)], min_val=1, max_val=GMAX)
                pe.wait_ge(s_ready, q)
                bank = ps_agg[:, bass.ds((q % 2) * CHUNK, CHUNK)]
                pe.matmul(bank, lhsT=zeros_h[0:1, 0:P], rhs=zeros_h[:], start=True, stop=False)
                if first:
                    pe.matmul(ps_deg[0:1, :], lhsT=zeros_h[0:1, 0:1], rhs=zeros_h[:], start=True, stop=False)
                with pe.Fori(start + n0, end + n0) as n:
                    pe.wait_ge(oh_ready, n)
                    for j in range(GROUP):
                        pe.wait_ge(gathered[0][j], ((n + 1) // 2) * 16 + 16 * PRIME)
                        pe.wait_ge(gathered[1][j], (n // 2) * 16 + 16 * PRIME)
                        g_at = (((n + 1) % 2) * GROUP + j) * (2 * H)
                        hot = OH[:, bass.ds(((n % (OHR // GROUP)) * GROUP + j) * CHUNK, CHUNK)]
                        pe.matmul(bank, lhsT=G[:, bass.ds(g_at, H)], rhs=hot, start=False, stop=False)
                        if first:
                            pe.matmul(ps_deg[0:1, :], lhsT=ones_h[:, 0:1], rhs=hot, start=False, stop=False)
                        mm = pe.matmul(bank, lhsT=G[:, bass.ds(g_at + H, H)], rhs=hot, start=False, stop=False)
                    mm.then_inc(groups_done, 1)
                if first:
                    pe.matmul(ps_deg[0:1, :], lhsT=zeros_h[0:1, 0:1], rhs=zeros_h[:], start=False, stop=True)
                pe.matmul(bank, lhsT=zeros_h[0:1, 0:P], rhs=zeros_h[:], start=False, stop=True).then_inc(agg_done, 1)

            def gates(q, c, before=True):
                pe.wait_ge(s_ready, q + 1)
                if before:
                    pe.wait_ge(t2_ready, q - 1)
                    pe.wait_ge(rz_ready, q - 1)
                cols = bass.ds(c * CHUNK, CHUNK)
                h_c, d_c = hT[:, cols], deg[0:1, cols]
                for g, bank in ((0, ps_r), (1, ps_z)):
                    w = slice(g * P, (g + 1) * P)
                    pe.matmul(bank[:], lhsT=wfT[:, w], rhs=S, start=True, stop=False)
                    pe.matmul(bank[:], lhsT=whhT[:, w], rhs=h_c, start=False, stop=False)
                    pe.matmul(bank[:], lhsT=cdeg[0:1, w], rhs=d_c, start=False, stop=True)
                w = slice(2 * P, 3 * P)
                pe.matmul(ps_hn[:], lhsT=whhT[:, w], rhs=h_c, start=True, stop=True)
                pe.matmul(ps_in[:], lhsT=wfT[:, w], rhs=S, start=True, stop=False)
                pe.matmul(ps_in[:], lhsT=cdeg[0:1, w], rhs=d_c, start=False, stop=True).then_inc(gates_done, 1)

            def turn(q):
                pe.wait_ge(h_ready, q + 1)
                pe.wait_ge(rows_copied, q)
                for b in range(4):
                    for a, part in enumerate((hi, lo)):
                        mm = pe.transpose(ps_rows[:, (2 * b + a) * P:(2 * b + a + 1) * P], part[:, b * P:(b + 1) * P], ident_h[:])
                mm.then_inc(rows_turned, 1)

            pe.sem_inc(s_ready, 1)
            total = pe.value_load(chunk_end[0:1, NCH:NCH + 1], min_val=1, max_val=GMAX)

            def step(s, first):
                n0 = pe.snap(s * total + 1) if not first else 1
                q0 = s * NCH + 1
                sums(q0, n0, 0, first)
                gates(q0, 0, before=not first)
                with pe.Fori(1, NCH) as c:
                    q = s * NCH + c + 1
                    sums(q, n0, c, first)
                    gates(q, c)
                    turn(q - 1)
                turn(s * NCH + NCH)

            step(0, True)
            with pe.Fori(1, STEPS) as s:
                step(s, False)

        @block.vector
        def _(dve):
            done = [0]

            def link(ins):
                done[0] += 1
                ins.then_inc(dve_step, 1)
                dve.wait_ge(dve_step, done[0])

            nc.vector.memset(src_sb[96:P, REM:K], NPAD - 1).then_inc(edges_padded, 1)
            nc.vector.memset(dst_sb[96:P, REM:K], 0).then_inc(edges_padded, 1)
            nc.vector.memset(fill[:], NO_NODE).then_inc(fill_ready, 1)
            dve.sem_inc(h_ready, 1)
            nc.vector.memset(ones_f[:], 1.0)
            nc.vector.memset(ones_h[:], 1.0)
            nc.vector.memset(zeros_h[:], 0.0)
            nc.vector.memset(hT[:], 0.0).then_inc(zeros_ready, 1)
            dve.wait_ge(iota_done, 2)
            nc.vector.tensor_copy(iota_h[:], iota_i[:])
            nc.vector.tensor_copy(iota_f[:], iota_i[:, 0:P])
            link(nc.vector.tensor_copy(part_f[:], part_i[:]))
            nc.vector.tensor_scalar(ident[:], iota_f[:], part_f[:, 0:1], None, ALU.is_equal)
            nc.vector.tensor_scalar(ident_h[:], iota_f[:], part_f[:, 0:1], None, ALU.is_equal)
            link(nc.vector.tensor_scalar(before[:], iota_f[:], part_f[:, 0:1], None, ALU.is_gt))
            nc.vector.memset(pos, 0.0).then_inc(pos_cleared, 1)
            dve.wait_ge(edges_loaded, 64)
            link(nc.vector.tensor_scalar(chunk_i, src_sb, 9, None, ALU.logical_shift_right))
            link(nc.vector.tensor_copy(chunk_b[:], chunk_i))
            link(nc.vector.tensor_scalar(chunk_i, src_sb, CHUNK - 1, None, ALU.bitwise_and))
            link(nc.vector.scalar_tensor_tensor(out=rec, in0=dst_sb, scalar=10, in1=chunk_i,
                                                op0=ALU.logical_shift_left, op1=ALU.bitwise_or))
            with dve.Fori(0, NCH) as b:
                nc.vector.tensor_scalar(mask[:], chunk_b[:], iota_f[:, bass.ds(b, 1)], None, ALU.is_equal).then_inc(mask_step, 1)
                dve.wait_ge(mask_step, b + 1)
                nc.vector.tensor_reduce(cnt[:, bass.ds(b, 1)], mask[:], AX_X, ALU.add).then_inc(rank_step, 1)
                dve.wait_ge(rank_step, b + 1)
            dve.drain().then_inc(counts_ready, 1)
            dve.wait_ge(prefix_ready, 1)
            link(nc.vector.tensor_scalar(grp_f[:], ps_r[:, 0:NCH], float(GE - 1), float(GE), ALU.add, ALU.max))
            link(nc.vector.tensor_copy(grp_i[:], grp_f[:]))
            shift = GE.bit_length() - 1
            link(nc.vector.tensor_scalar(grp_i[:], grp_i[:], shift, None, ALU.logical_shift_right))
            link(nc.vector.tensor_copy(grp_f[:], grp_i[:]))
            link(nc.vector.tensor_copy(cum[:, 0, :], grp_i[:]))
            a, d = 0, 1
            while d < NCH:
                nc.vector.tensor_copy(cum[:, 1 - a, 0:d], cum[:, a, 0:d])
                link(nc.vector.tensor_tensor(cum[:, 1 - a, d:NCH], cum[:, a, d:NCH], cum[:, a, 0:NCH - d], ALU.add))
                a, d = 1 - a, 2 * d
            link(nc.vector.tensor_tensor(start_f[:], cum[:, a, :], grp_f[:], ALU.subtract))
            nc.vector.tensor_copy(chunk_end[:, 0:NCH], start_f[:])
            link(nc.vector.tensor_scalar(chunk_end[:, NCH:NCH + 1], cum[:, a, NCH - 1:NCH], float(ISETS - 1), None, ALU.add))
            link(nc.vector.tensor_scalar(chunk_end[:, NCH:NCH + 1], chunk_end[:, NCH:NCH + 1], 0x7FFFFFFF - (ISETS - 1), None, ALU.bitwise_and))
            link(nc.vector.tensor_scalar(base[:], start_f[:], float(GE), None, ALU.mult))
            link(nc.vector.tensor_tensor(base[:], base[:], ps_z[:, 0:NCH], ALU.add))
            with dve.Fori(1, NCH + 1) as b:
                nc.vector.tensor_scalar(mask[:], chunk_b[:], iota_f[:, bass.ds(b - 1, 1)], None, ALU.is_equal).then_inc(chunk_masked, 1)
                dve.wait_ge(chunk_masked, b)
                nc.vector.tensor_tensor_scan(scan, mask[:], mask[:], base[:, bass.ds(b - 1, 1)], ALU.add, ALU.max).then_inc(chunk_ranked, 1)
                dve.wait_ge(pos_cleared, 1)
                dve.wait_ge(chunk_ranked, b)
                nc.vector.copy_predicated(pos, mask[:], scan).then_inc(chunk_placed, 1)
                dve.wait_ge(chunk_placed, b)
            link(nc.vector.tensor_scalar(pos_i, pos, -1.0, None, ALU.add))
            link(nc.vector.tensor_scalar(pos_hi, pos_i, 7, None, ALU.logical_shift_right))
            link(nc.vector.tensor_scalar(pos_i, pos_i, P - 1, None, ALU.bitwise_and))
            link(nc.vector.scalar_tensor_tensor(out=pos, in0=pos_i, scalar=float(T), in1=pos_hi, op0=ALU.mult, op1=ALU.add))
            nc.vector.tensor_copy(pos_i, pos).then_inc(pos_ready, 1)
            dve.wait_ge(w_turned, 1)
            nc.vector.tensor_copy(wihT[:], ps_in[:, 0:3 * P])
            nc.vector.tensor_copy(whhT[:], ps_hn[:, 0:3 * P]).then_inc(w_copied, 1)
            dve.wait_ge(w_turned, 2)
            nc.vector.tensor_copy(wfT[:], ps_in[:, 0:3 * P])
            nc.vector.tensor_copy(cdeg[:], ps_hn[0:1, 0:3 * P]).then_inc(w_copied, 1)
            nc.vector.tensor_tensor(bsum[:], bih_sb[:], bhh_sb[:], ALU.add).then_inc(w_copied, 1)
            loaded = [0, 0]
            for g in range(NLN):
                loaded[g % 2] += 16 * PIECES[g]
                xt = xg[:, g % 2]
                dve.wait_ge(x_loaded[g % 2], loaded[g % 2])
                for t in range(LNT):
                    link(nc.vector.bn_stats(stats[:], xt[:, t, :]))
                    link(nc.vector.bn_aggr(mv[:, t, :], stats[:]))
                link(nc.vector.tensor_scalar(mv[:, :, 1], mv[:, :, 1], EPS, None, ALU.add))
                dve.sem_inc(var_ready, 1)
                dve.wait_ge(std_ready, g + 1)
                link(nc.vector.reciprocal(rstd[:], std[:]))
                for t in range(LNT):
                    last = nc.vector.tensor_scalar(xt[:, t, :], xt[:, t, :], mv[:, t, 0:1], rstd[:, t:t + 1], ALU.subtract, ALU.mult)
                link(last)
                link(nc.vector.tensor_scalar(xt, xt, 0.0, None, ALU.max))
                if g >= 1:
                    dve.wait_ge(rows_stored, 16 * g)
                link(nc.vector.tensor_scalar(lnrow[:, :, 0, :], xt, SCALE, None, ALU.mult))
                nc.vector.scalar_tensor_tensor(out=lnrow[:, :, 1, :], in0=xt, scalar=SCALE, in1=lnrow[:, :, 0, :],
                                               op0=ALU.mult, op1=ALU.subtract).then_inc(ln_rows_ready, 1)
                dve.wait_ge(zeros_stored, 32)
                for t in range(LNT):
                    n = g * LNT + t
                    dve.wait_ge(lnT_ready, n + 1)
                    nc.vector.tensor_copy(hT[:, n * P:(n + 1) * P],
                                          ps_agg[:, (n % 2) * CHUNK:(n % 2) * CHUNK + P]).then_inc(lnT_copied, 1)
            dve.wait_ge(rec_loaded, 16)
            nc.vector.tensor_scalar(idx_tab[:, 0:T], rec_sb[:], 10, None, ALU.logical_shift_right)
            link(nc.vector.tensor_scalar(rec_sb[:], rec_sb[:], NO_NODE, None, ALU.bitwise_and))
            nc.vector.tensor_copy(loc_tab, rec_sb[:])
            link(nc.vector.tensor_scalar(idx_tab[:, T:2 * T], idx_tab[:, 0:T], float(NPAD), None, ALU.add))
            dve.drain().then_inc(tables_ready, 1)
            total = dve.value_load(chunk_end[0:1, NCH:NCH + 1], min_val=1, max_val=GMAX)

            def hots(n0, c):
                start = dve.value_load(chunk_end[0:1, bass.ds(c, 1)], min_val=0, max_val=GMAX)
                end = dve.value_load(chunk_end[0:1, bass.ds(c + 1, 1)], min_val=1, max_val=GMAX)
                with dve.Fori(start, end) as g:
                    n = dve.snap(g + n0)
                    dve.wait_ge(groups_done, n + 1)
                    for j in range(GROUP):
                        hot = OH[:, bass.ds(((n % (OHR // GROUP)) * GROUP + j) * CHUNK, CHUNK)]
                        ins = nc.vector.tensor_scalar(hot, iota_h[:], loc_tab[:, bass.ds(g * GROUP + j, 1)], None, ALU.is_equal)
                    ins.then_inc(oh_ready, 1)

            def update(q, c):
                h_c = hT[:, bass.ds(c * CHUNK, CHUNK)]
                dve.wait_ge(rz_ready, q)
                nc.vector.scalar_tensor_tensor(out=t_sb[:], in0=ps_hn[:], scalar=bhh_sb[:, 2:3], in1=r_sb,
                                               op0=ALU.add, op1=ALU.mult).then_inc(t_done, 1)
                dve.wait_ge(t_done, q)
                nc.vector.tensor_tensor(t_sb[:], ps_in[:], t_sb[:], ALU.add).then_inc(t2_ready, 1)
                dve.wait_ge(n_ready, q)
                nc.vector.tensor_tensor(t_sb[:], h_c, n_sb[:], ALU.subtract).then_inc(upd_step, 1)
                dve.wait_ge(upd_step, q * 4 - 3)
                nc.vector.tensor_tensor(t_sb[:], t_sb[:], z_sb, ALU.mult).then_inc(upd_step, 1)
                dve.wait_ge(upd_step, q * 4 - 2)
                nc.vector.tensor_tensor(h_c, n_sb[:], t_sb[:], ALU.add).then_inc(upd_step, 1)
                dve.wait_ge(upd_step, q * 4 - 1)
                dve.wait_ge(rows_turned, q)
                nc.vector.tensor_scalar(hi[:], h_c, SCALE, None, ALU.mult).then_inc(upd_step, 1)
                dve.wait_ge(upd_step, q * 4)
                nc.vector.scalar_tensor_tensor(out=lo[:], in0=h_c, scalar=SCALE, in1=hi[:],
                                               op0=ALU.mult, op1=ALU.subtract).then_inc(h_ready, 1)

            with dve.Fori(0, STEPS) as s:
                n0 = dve.snap(s * total + 1)
                hots(n0, 0)
                with dve.Fori(1, NCH) as c:
                    hots(n0, c)
                    update(s * NCH + c, c - 1)
                update(s * NCH + NCH, NCH - 1)
            loaded = [0, 0]
            for g in range(NLN):
                loaded[g % 2] += 16 * (1 + PIECES[g])
                dve.wait_ge(fin_rows[g % 2], loaded[g % 2])
                rows, xt = fin_bufs(g % 2), xg[:, g % 2]
                for part in range(2):
                    ins = nc.vector.scalar_tensor_tensor(out=xt, in0=rows[:, :, part * H:(part + 1) * H], scalar=1.0 / SCALE,
                                                         in1=xt, op0=ALU.mult, op1=ALU.add)
                    if part == 0:
                        link(ins)
                ins.then_inc(fin_ready, 1)


_INS = ["x", "src", "dst", "L0_gnn_W_msg", "L0_gnn_b_msg", "L0_gnn_W_ih", "L0_gnn_W_hh", "L0_gnn_b_ih", "L0_gnn_b_hh"]


def kernel(**inputs):
    import numpy as _np
    import concourse.bacc as _bacc
    from concourse import mybir as _mybir
    from concourse.bass_utils import run_bass_kernel_spmd as _run

    nc = _bacc.Bacc("TRN2", target_bir_lowering=False, num_devices=1)
    arrays, args = {}, []
    for name in _INS:
        a = _np.ascontiguousarray(inputs[name])
        arrays[f"in_{name}_dram"] = a
        args.append(nc.dram_tensor(f"in_{name}_dram", a.shape, _mybir.dt.from_np(a.dtype), kind="ExternalInput").ap())
    shape = inputs["x"].shape
    args.append(nc.dram_tensor("out_0_dram", shape, _mybir.dt.float32, kind="ExternalOutput").ap())
    build_gnn(nc, *args)
    r = _run(nc, [arrays], core_ids=[0])
    return r.results[0]["out_0_dram"]
```

```python
from contextlib import ExitStack

import concourse.bass as bass
from concourse import mybir

ALU = mybir.AluOpType
ACT = mybir.ActivationFunctionType
AX_X = mybir.AxisListType.X
F32 = mybir.dt.float32
F16 = mybir.dt.float16
BF16 = mybir.dt.bfloat16
I32 = mybir.dt.int32
U16 = mybir.dt.uint16

P = 128
STEPS = 5
CHUNK = 512
GROUP = 4
ISETS = 4
PRIME = ISETS // 2
OHR = 4 * GROUP
SCALE = 2048.0
EPS = 1e-5
SC_HALF = 8
NO_NODE = 1023


def build_fast(nc, ctx, flag_out, x, src, dst, W_msg, b_msg, W_ih, W_hh, b_ih, b_hh, out):
    N, H = x.shape
    E = src.shape[0]
    assert H == P
    NCH = -(-N // CHUNK)
    NPAD = NCH * CHUNK
    NT = -(-N // P)
    HALF = CHUNK // 2
    assert 0 < N - (NCH - 1) * CHUNK < HALF
    ND = NCH // 2
    NG = NCH - ND
    NH = 2 * NG - 1
    K = -(-E // (P * 2 * SC_HALF)) * 2 * SC_HALF
    FULL = E // K
    REM = E - FULL * K
    assert FULL == P - 1 and REM > 0
    OWN = CHUNK // P
    DT = NT + OWN
    SETS = 6
    TS = 6
    HT = SETS * TS
    G0 = ND * DT
    T = G0 + NH * HT
    REL = 3
    NKEY = ND * REL + NH
    CUTS = [0, K // 8, K // 4, K // 2, K]
    TURNS = K // (2 * SC_HALF)
    UNITS = 8
    DSETS = 2 * SETS
    TAIL = NT - DSETS * UNITS
    assert 0 < TAIL <= 2 and NT <= P
    RING = 3
    UW = UNITS * CHUNK
    HB = 8
    NW = NPAD // P
    LNT = 14
    assert NT % LNT == 0 and K % (16 * SC_HALF) == 0
    NLN = NT // LNT
    NFULL = N // P
    NREM = N - NFULL * P
    PAD_NODE = (NCH - 1) * CHUNK + HALF - 1
    assert PAD_NODE >= N

    rec_dram = nc.dram_tensor("fast_rec", (P * T, 1), I32, kind="Internal").ap()
    hrows = nc.dram_tensor("fast_hrows", (2 * NPAD, 2 * H), F16, kind="Internal").ap()
    adj = nc.dram_tensor("fast_adj", (ND * DSETS * P, UW), F16, kind="Internal").ap()
    adj_tail = nc.dram_tensor("fast_adj_tail", (ND * P, TAIL * CHUNK), F16, kind="Internal").ap()
    deg_dram = nc.dram_tensor("fast_deg", (9, NPAD), BF16, kind="Internal").ap()
    c9_dram = nc.dram_tensor("fast_c9", (9, 3 * P), BF16, kind="Internal").ap()

    steps_only = {}

    def sem(name):
        return ctx.enter_context(nc.semaphore("fast_" + name))

    def step_sem(name):
        steps_only[name] = ctx.enter_context(nc.semaphore(name))
        return steps_only[name]

    with ExitStack() as mem:
        def sb(name, shape, dt):
            return mem.enter_context(nc.sbuf_tensor("f_" + name, shape, dt))

        def psum(name, shape, dt):
            return mem.enter_context(nc.psum_tensor("f_" + name, shape, dt))

        ps_d = psum("ps_d", [P, CHUNK], F32)
        ps_g = psum("ps_g", [P, CHUNK], F32)
        ps_r = psum("ps_r", [P, CHUNK], F32)
        ps_z = psum("ps_z", [P, CHUNK], F32)
        ps_in = psum("ps_in", [P, CHUNK], F32)
        ps_hn = psum("ps_hn", [P, CHUNK], F32)
        ps_rows = psum("ps_rows", [P, 8 * P], F16)
        ps_deg = psum("ps_deg", [P, CHUNK], F32)

        room = sb("room", [P, NT * 2 * H // 2], I32)
        src_sb = room[:, 0:K]
        dst_sb = room[:, K:2 * K]
        tmp_i = room[:, 2 * K:3 * K]
        tmp_f = room[:, 3 * K:4 * K].bitcast(F32)
        pos = room[:, 4 * K:5 * K].bitcast(F32)
        pos_i = room[:, 5 * K:6 * K]
        rec = room[:, 6 * K:7 * K]
        loc_f = src_sb.bitcast(F32)
        win_f = dst_sb.bitcast(F32)
        ohs = room[:, 0:2 * 12 * CHUNK // 2].bitcast(F16)
        ohd = room[:, 12 * CHUNK:12 * CHUNK + 2 * 12 * P // 2].bitcast(F16)
        stage = room[:, 8192:8192 + UW].bitcast(F16)
        hr = room[:].bitcast(F16)
        room2 = sb("room2", [P, (RING * UW + TAIL * CHUNK) // 2], I32)
        key_b = room2[:, 0:K // 2].bitcast(BF16)
        mask = room2[:, K // 2:K].bitcast(U16)
        hots = room2[:, K:K + 4 * HB * P // 2].bitcast(BF16)
        hot_l = [hots[:, a * HB * P:(a + 1) * HB * P] for a in range(2)]
        hot_w = [hots[:, a * HB * P:(a + 1) * HB * P] for a in range(2, 4)]
        a_ring = room2[:, 0:RING * UW // 2].bitcast(F16)
        a_tail = room2[:, RING * UW // 2:].bitcast(F16)
        st_tail = room[:, 7680:7680 + TAIL * CHUNK // 2].bitcast(F16)
        assert K + 2 * HB * P <= (RING * UW) // 2 and 12 * CHUNK + 12 * P <= 7680 and 7680 + TAIL * CHUNK // 2 <= 8192 and 8192 + UW <= NT * H
        hT = sb("hT", [P, NPAD], F32)
        rec_sb = sb("rec_sb", [P, T], I32)
        idx_tab = sb("idx_tab", [P, 2 * NH * HT], I32)
        loc_g = sb("loc_g", [P, NH * HT], F32)
        xg = sb("xg", [P, 2, LNT, P], F32)
        xflat = xg[:].rearrange("p a t k -> p (a t k)")
        loc_d = xflat[:, 0:G0]
        dst_d = xflat[:, G0:2 * G0]
        lnrow = sb("lnrow", [P, LNT, 2, P], F16)
        srz = lnrow[:].rearrange("p t a k -> p (t a k)").bitcast(F32)
        S_g = srz[:, 0:CHUNK]
        r_sb = srz[:, CHUNK:2 * CHUNK]
        z_sb = srz[:, 2 * CHUNK:3 * CHUNK]
        S_d = sb("S_d", [P, CHUNK], F32)
        t_sb = sb("t_sb", [P, CHUNK], F32)
        n_sb = sb("n_sb", [P, CHUNK], F32)
        hi = sb("hi", [P, CHUNK], F16)
        lo = sb("lo", [P, CHUNK], F16)
        G = sb("G", [P, RING * TS * 2 * H], F16)
        OH = sb("OH", [P, RING * TS * HALF], F16)
        idx_slot = sb("idx_slot", [P, HT], I32)
        sc_pos = sb("sc_pos", [P, 2 * SC_HALF], I32)
        sc_rec = sb("sc_rec", [P, 2 * SC_HALF], I32)
        iota_i = sb("iota_i", [P, CHUNK], I32)
        rowbuf = iota_i[:].bitcast(F16)
        iota_h = sb("iota_h", [P, CHUNK], F16)
        iota_b = sb("iota_b", [P, P], BF16)
        iota_f = sb("iota_f", [P, P], F32)
        part_i = sb("part_i", [P, 1], I32)
        part_f = sb("part_f", [P, 1], F32)
        ident = sb("ident", [P, P], F32)
        ident_h = sb("ident_h", [P, P], F16)
        early_o = OH[:].bitcast(F32)
        before = early_o[:, 0:P]
        after1 = early_o[:, P:2 * P]
        ones_f = early_o[:, 2 * P:3 * P]
        zeros_h = sb("zeros_h", [1, CHUNK], F16)
        cnt = sb("cnt", [P, NKEY], F32)
        base = sb("base", [P, NKEY], F32)
        early_g = G[:].bitcast(F32)
        at_win = early_g[:, 0:REL * NT].rearrange("p (k j) -> p k j", k=REL)
        past_win = early_g[:, REL * NT:2 * REL * NT].rearrange("p (k j) -> p k j", k=REL)
        at_winT = early_g[:, 2 * REL * NT:2 * REL * NT + REL * P].rearrange("p (k q) -> p k q", k=REL)
        tb = sb("tb", [P, 4, ND], F32)
        small = sb("small", [P, 8], F32)
        bad = sb("bad", [P, 8], F32)
        flag_sb = sb("flag_sb", [1, 1], I32)
        w_at = 2 * REL * NT + REL * P
        wmsg_sb = early_g[:, w_at:w_at + P]
        wih_sb = early_g[:, w_at + P:w_at + 4 * P].rearrange("p (g k) -> p g k", g=3)
        whh_sb = early_g[:, w_at + 4 * P:w_at + 7 * P].rearrange("p (g k) -> p g k", g=3)
        wihT = sb("wihT", [P, 3 * P], F32)
        whhT = sb("whhT", [P, 3 * P], F32)
        wfT = sb("wfT", [P, 3 * P], F32)
        cdeg = early_g[0:1, w_at + 7 * P:w_at + 10 * P]
        cpart = early_o[0:1, 3 * P:3 * P + 9 * P // 2].bitcast(BF16).rearrange("p (a k) -> p a k", a=3)
        c9 = sb("c9", [9, 3 * P], BF16)
        bmsg_sb = sb("bmsg_sb", [P, 1], F32)
        bih_sb = sb("bih_sb", [P, 3], F32)
        bhh_sb = sb("bhh_sb", [P, 3], F32)
        bsum = sb("bsum", [P, 3], F32)
        deg_f = S_d
        dpart = t_sb[:].bitcast(BF16)
        deg9 = [sb("deg9_0", [9, CHUNK], BF16), sb("deg9_1", [9, CHUNK], BF16)]
        stats = sb("stats", [P, 6], F32)
        mv = sb("mv", [P, LNT, 2], F32)
        std = sb("std", [P, LNT], F32)
        rstd = sb("rstd", [P, LNT], F32)

        edges_padded = sem("edges_padded")
        edges_loaded = sem("edges_loaded")
        fill_ready = sem("fill_ready")
        rec_filled = sem("rec_filled")
        zeros_ready = sem("zeros_ready")
        zeros_stored = sem("zeros_stored")
        weights_loaded = sem("weights_loaded")
        iota_done = sem("iota_done")
        dve_step = sem("dve_step")
        keys_counted = sem("keys_counted")
        counts_ready = sem("counts_ready")
        prefix_ready = sem("prefix_ready")
        windows_turned = sem("windows_turned")
        windows_copied = sem("windows_copied")
        slots_based = sem("slots_based")
        base_picked = sem("base_picked")
        bad_ready = sem("bad_ready")
        bad_summed = sem("bad_summed")
        flag_ready = sem("flag_ready")
        flag_stored = sem("flag_stored")
        key_masked = sem("key_masked")
        key_ranked = sem("key_ranked")
        key_placed = sem("key_placed")
        key_carried = sem("key_carried")
        pos_ready = sem("pos_ready")
        slots_filled = [sem("slots_filled_0"), sem("slots_filled_1")]
        scattered = [sem("scattered_0"), sem("scattered_1")]
        pool_turns = sem("pool_turns")
        sp_turns = step_sem("sp_turns")
        pe_turns = step_sem("pe_turns")
        hot_ready = sem("hot_ready")
        hot_used = sem("hot_used")
        deg_parts = sem("deg_parts")
        deg_stored = sem("deg_stored")
        c_parts = sem("c_parts")
        c9_stored = sem("c9_stored")
        c9_loaded = sem("c9_loaded")
        rec_loaded = sem("rec_loaded")
        tables_ready = sem("tables_ready")
        x_loaded = [sem("x_loaded_0"), sem("x_loaded_1")]
        var_ready = sem("var_ready")
        std_ready = sem("std_ready")
        lnT_ready = sem("lnT_ready")
        lnT_copied = sem("lnT_copied")
        ln_rows_ready = sem("ln_rows_ready")
        rows_stored = sem("rows_stored")
        w_turned = sem("w_turned")
        w_copied = sem("w_copied")
        set_hot = step_sem("set_hot")
        unit_built = step_sem("unit_built")
        evac_act = step_sem("evac_act")
        evac_dve = step_sem("evac_dve")
        stage_free = [sem("stage_free_0"), sem("stage_free_1"), sem("stage_free_2")]
        a_stored = [sem("a_stored_0"), sem("a_stored_1"), sem("a_stored_2")]
        a_loaded = [sem(f"a_loaded_{i}") for i in range(RING)]
        tail_loaded = step_sem("tail_loaded")
        dense_done = step_sem("dense_done")
        tails_done = step_sem("tails_done")
        rows_loaded = step_sem("rows_loaded")
        deg9_loaded = [sem("deg9_loaded_0"), sem("deg9_loaded_1")]
        idx_loaded = [step_sem(f"idx_loaded_{i}") for i in range(SETS)]
        gathered = [[step_sem(f"gathered_{a}_{j}") for j in range(TS)] for a in range(RING)]
        oh_ready = step_sem("oh_ready")
        sets_done = step_sem("sets_done")
        agg_done = step_sem("agg_done")
        s_ready = step_sem("s_ready")
        gates_done = step_sem("gates_done")
        rz_ready = step_sem("rz_ready")
        t_done = step_sem("t_done")
        t2_ready = step_sem("t2_ready")
        n_ready = step_sem("n_ready")
        upd_step = step_sem("upd_step")
        h_ready = step_sem("h_ready")
        rows_turned = step_sem("rows_turned")
        rows_copied = step_sem("rows_copied")
        fin_rows = [step_sem("fin_rows_0"), step_sem("fin_rows_1")]
        fin_ready = step_sem("fin_ready")
        out_stored = step_sem("out_stored")

        def x_tiles(t, g, first):
            lo_row = g * LNT * P
            n_full = min(LNT, NFULL - g * LNT)
            pieces = [(t[lo_row:lo_row + n_full * P, :].rearrange("(t p) f -> p t f", p=P), first[:, 0:n_full, :])]
            if n_full < LNT:
                pieces.append((t[NFULL * P:N, :], first[0:NREM, n_full, :]))
            return pieces

        PIECES = [len(x_tiles(x, g, xg[:, 0])) for g in range(NLN)]

        def fin_bufs(b):
            return room[:, b * LNT * P:(b + 1) * LNT * P].bitcast(F16).rearrange("p (t k) -> p t k", k=2 * H)

        def build_sets(eng, one):
            one(0, 0, UNITS, 0)
            with eng.Fori(0, (DSETS - 2) // 2) as bb:
                one(bb * 2 + 1, bb * (2 * UNITS) + UNITS + OWN, UNITS, 1)
                one(bb * 2 + 2, bb * (2 * UNITS) + 2 * UNITS + OWN, UNITS, 0)
            one(DSETS - 1, (DSETS - 1) * UNITS + OWN, UNITS, 1)
            one(DSETS, DSETS * UNITS + OWN, TAIL, 2)

        def gathered_chunk(mi):
            return (mi + ND) % (ND + 1) + ND

        def unit_tiles(b, v):
            if b is 0:
                return [2 * v, 2 * v + 1] if v < OWN else [v + OWN]
            return [v]

        ACT_UNITS = list(range(UNITS - 1))
        ACT_CHUNK = DSETS * len(ACT_UNITS) + TAIL
        DVE_CHUNK = DSETS * (UNITS - len(ACT_UNITS))

        def unit_bank(v, par):
            if par == 2:
                return (ps_d, ps_g)[v]
            return (ps_r, ps_z, ps_in, ps_hn)[v % 4] if v in ACT_UNITS else ps_deg

        block = mem.enter_context(nc.Block())

        def store_ln(sp, g):
            sp.wait_ge(ln_rows_ready, g + 1)
            at = g * LNT * P
            sp.dma_start(hrows[at:at + LNT * P, :].rearrange("(t p) k -> p t k", p=P),
                         lnrow[:].rearrange("p t a k -> p t (a k)")).then_inc(rows_stored, 16)

        def store_out(sp, g):
            sp.wait_ge(fin_ready, g + 1)
            for rows, tile in x_tiles(out, g, xg[:, g % 2]):
                sp.dma_start(rows, tile).then_inc(out_stored, 16)

        @block.sync
        def _(sp):
            sp.wait_ge(edges_padded, 2)
            for flat, tile in ((src, src_sb), (dst, dst_sb)):
                sp.dma_start(tile[0:FULL, :], flat[0:FULL * K].rearrange("(p k) -> p k", k=K)).then_inc(edges_loaded, 16)
                sp.dma_start(tile[FULL:P, 0:REM], flat[FULL * K:E].rearrange("(a k) -> a k", a=1)).then_inc(edges_loaded, 16)
            sp.wait_ge(fill_ready, 1)
            sp.dma_start(rec_dram.rearrange("(p t) o -> p (t o)", p=P), rec_sb[:]).then_inc(rec_filled, 16)
            sp.dma_start(wmsg_sb, W_msg).then_inc(weights_loaded, 16)
            sp.dma_start(wih_sb[:], W_ih.rearrange("(g p) k -> p g k", p=P)).then_inc(weights_loaded, 16)
            sp.dma_start(whh_sb[:], W_hh.rearrange("(g p) k -> p g k", p=P)).then_inc(weights_loaded, 16)
            sp.dma_start(bmsg_sb[:], b_msg.rearrange("(p o) -> p o", o=1)).then_inc(weights_loaded, 16)
            for g in range(3):
                sp.dma_start(bih_sb[:, g:g + 1], b_ih[g * P:(g + 1) * P].rearrange("(p o) -> p o", o=1)).then_inc(weights_loaded, 16)
                sp.dma_start(bhh_sb[:, g:g + 1], b_hh[g * P:(g + 1) * P].rearrange("(p o) -> p o", o=1)).then_inc(weights_loaded, 16)
            sp.wait_ge(zeros_ready, 1)
            zeros = hT[:].bitcast(F16)
            sp.dma_start(hrows[NPAD:2 * NPAD, :].rearrange("(p r) k -> p (r k)", p=P), zeros).then_inc(zeros_stored, 16)
            sp.dma_start(hrows[NT * P:NPAD, :].rearrange("(p r) k -> p (r k)", p=P),
                         zeros[:, 0:(NPAD - NT * P) // P * 2 * H]).then_inc(zeros_stored, 16)
            sp.wait_ge(flag_ready, 1)
            sp.dma_start(flag_out, flag_sb[:]).then_inc(flag_stored, 16)
            sp.wait_ge(c_parts, 1)
            for b in range(3):
                sp.dma_start(c9_dram.rearrange("(a b) k -> b a k", b=3)[b:b + 1], cpart).then_inc(c9_stored, 16)
            sp.wait_ge(c9_stored, 48)
            sp.dma_start(c9[:], c9_dram).then_inc(c9_loaded, 16)
            sp.wait_ge(deg_parts, 1)
            for r in range(9):
                sp.dma_start(deg_dram[r, :].rearrange("(w l) -> w l", l=P),
                             dpart[0:NW, (r % 3) * P:(r % 3 + 1) * P]).then_inc(deg_stored, 16)
            sp.wait_ge(deg_stored, 16 * 9)
            for g in range(NLN):
                if g >= 2:
                    sp.wait_ge(ln_rows_ready, g - 1)
                    sp.wait_ge(lnT_copied, (g - 1) * LNT)
                for rows, tile in x_tiles(x, g, xg[:, g % 2]):
                    sp.dma_start(tile, rows).then_inc(x_loaded[g % 2], 16)
                if g >= 1:
                    store_ln(sp, g - 1)
            store_ln(sp, NLN - 1)
            for h in range(2):
                sp.wait_ge(scattered[h], 16 * SC_HALF * TURNS)
            sp.dma_start(rec_sb[:], rec_dram.rearrange("(p t) o -> p (t o)", p=P)).then_inc(rec_loaded, 16)
            sp.wait_ge(rec_loaded, 16)
            sp.wait_ge(flag_stored, 16)
            fast = sp.value_load(flag_sb[0:1, 0:1], min_val=0, max_val=1)
            with sp.If(fast > 0):
                with sp.Fori(0, ND) as mi:
                    def one(b, tile0, units, par):
                        if par == 2:
                            sp.wait_ge(evac_act, mi * ACT_CHUNK + ACT_CHUNK + 3)
                            sp.sem_inc(sp_turns, 1)
                            sp.dma_start(adj_tail[bass.ds(mi * P, P), :], st_tail).then_inc(a_stored[2], 16)
                            sp.wait_ge(a_stored[1], mi * (8 * DSETS) + 8 * DSETS)
                            sp.sem_inc(stage_free[1], 1)
                            sp.wait_ge(a_stored[2], mi * 16 + 16)
                            sp.sem_inc(stage_free[2], 1)
                            return
                        sp.wait_ge(evac_act, mi * ACT_CHUNK + b * len(ACT_UNITS) + (len(ACT_UNITS) + 3))
                        sp.sem_inc(sp_turns, 1)
                        sp.wait_ge(evac_dve, mi * DVE_CHUNK + b * (UNITS - len(ACT_UNITS)) + (UNITS - len(ACT_UNITS) + 1))
                        sp.sem_inc(sp_turns, 1)
                        at = ((mi * DSETS + b) * P).with_bounds(max_val=(ND * DSETS - 1) * P)
                        sp.dma_start(adj[bass.ds(at, P), :], stage[:, par * UW:(par + 1) * UW]).then_inc(a_stored[par], 16)
                        if b is not 0:
                            if par:
                                sp.wait_ge(a_stored[0], mi * (8 * DSETS) + (b + 1) * 8)
                            else:
                                sp.wait_ge(a_stored[1], mi * (8 * DSETS) + b * 8)
                            sp.sem_inc(stage_free[1 - par], 1)

                    build_sets(sp, one)
                def load_idx(i, h_next, par):
                    at = (par * (NH * HT) + h_next * HT + i * TS).with_bounds(max_val=2 * NH * HT - TS)
                    sp.dma_start(idx_slot[:, i * TS:(i + 1) * TS], idx_tab[:, bass.ds(at, TS)]).then_inc(idx_loaded[i], 16)

                def next_idx(h, i):
                    for j in range(TS):
                        sp.wait_ge(gathered[i % RING][j], h * 32 + (16 * (i // RING + 1) - 32))
                    sp.sem_inc(sp_turns, 1)
                    load_idx(i, (h + (NH - 1)) % NH, (h // NH) % 2)

                def load_a(number, slot):
                    at = ((number % (ND * DSETS)) * P).with_bounds(max_val=(ND * DSETS - 1) * P)
                    sp.dma_start(a_ring[:, slot * UW:(slot + 1) * UW], adj[bass.ds(at, P), :]).then_inc(a_loaded[slot], 16)

                for i in range(SETS):
                    sp.dma_start(idx_slot[:, i * TS:(i + 1) * TS], idx_tab[:, (NH - 1) * HT + i * TS:(NH - 1) * HT + (i + 1) * TS]).then_inc(idx_loaded[i], 16)
                for i in range(2):
                    sp.dma_start(a_ring[:, i * UW:(i + 1) * UW], adj[i * P:(i + 1) * P, :]).then_inc(a_loaded[i], 16)
                with sp.Fori(0, STEPS) as s:
                    sp.wait_ge(rows_stored, s * (16 * NCH) + 16 * NLN)
                    sp.sem_inc(sp_turns, 1)
                    for g in range(NLN):
                        at = (s % 2) * NPAD + g * LNT * P
                        sp.dma_start(hr[:, g * LNT * 2 * H:(g + 1) * LNT * 2 * H].rearrange("p (t k) -> p t k", t=LNT),
                                     hrows[bass.ds(at, LNT * P), :].rearrange("(t p) k -> p t k", p=P)).then_inc(rows_loaded, 16)
                    sp.dma_start(deg9[1][:], deg_dram[:, (NCH - 1) * CHUNK:NCH * CHUNK]).then_inc(deg9_loaded[1], 16)

                    for i in range(SETS):
                        next_idx(s * NH + 1, i)
                    with sp.Fori(0, ND) as mi:
                        q = s * NCH + mi * 2 + 2
                        sp.wait_ge(tails_done, s * ND + mi + 1)
                        sp.sem_inc(sp_turns, 1)
                        sp.dma_start(a_tail, adj_tail[bass.ds(mi * P, P), :]).then_inc(tail_loaded, 16)
                        for half in range(2):
                            for i in range(SETS):
                                a = s * (ND * DSETS) + mi * DSETS + half * SETS + i
                                sp.wait_ge(dense_done, a + 1)
                                sp.sem_inc(sp_turns, 1)
                                load_a(a + 2, (i + 2) % RING)
                                next_idx(s * NH + mi * 2 + (half + 2), i)
                            if half == 0:
                                sp.wait_ge(gates_done, q - 1)
                                sp.sem_inc(sp_turns, 1)
                                sp.dma_start(deg9[0][:], deg_dram[:, bass.ds(mi * CHUNK, CHUNK)]).then_inc(deg9_loaded[0], 16)
                                sp.dma_start(deg9[1][:], deg_dram[:, bass.ds(mi * CHUNK + ND * CHUNK, CHUNK)]).then_inc(deg9_loaded[1], 16)
                sp.wait_ge(rows_stored, 16 * (NLN + STEPS * NCH))
                for i in range(2):
                    sp.wait_ge(a_loaded[i], 16 * (STEPS * ND * DSETS // RING + 1))
                for i in range(SETS):
                    sp.wait_ge(idx_loaded[i], 16 * (STEPS * NH + 1))
                par = STEPS % 2
                for g in range(NLN):
                    if g >= 2:
                        sp.wait_ge(fin_ready, g - 1)
                        sp.wait_ge(out_stored, 16 * sum(PIECES[:g - 1]))
                    at = par * NPAD + g * LNT * P
                    sp.dma_start(fin_bufs(g % 2), hrows[at:at + LNT * P, :].rearrange("(t p) k -> p t k", p=P)).then_inc(fin_rows[g % 2], 16)
                    for rows, tile in x_tiles(x, g, xg[:, g % 2]):
                        sp.dma_start(tile, rows).then_inc(fin_rows[g % 2], 16)
                    if g >= 1:
                        store_out(sp, g - 1)
                store_out(sp, NLN - 1)
                sp.wait_ge(out_stored, 16 * sum(PIECES))

        @block.gpsimd
        def _(pool):
            nc.gpsimd.iota(iota_i[:], pattern=[[1, CHUNK]], base=0, channel_multiplier=0).then_inc(iota_done, 1)
            nc.gpsimd.iota(part_i[:], pattern=[[0, 1]], base=0, channel_multiplier=1).then_inc(iota_done, 1)
            pool.wait_ge(rec_filled, 16)
            with pool.Fori(1, TURNS + 1) as i:
                for h in range(2):
                    pool.wait_ge(slots_filled[h], i)
                    pool.sem_inc(pool_turns, 1)
                    for j in range(h * SC_HALF, (h + 1) * SC_HALF):
                        nc.gpsimd.indirect_dma_start(
                            rec_dram, bass.IndirectOffsetOnAxis(ap=sc_pos[:, j:j + 1], axis=0),
                            sc_rec[:, j:j + 1], None).then_inc(scattered[h], 16)
            pool.wait_ge(flag_ready, 1)
            pool.wait_ge(zeros_stored, 32)
            fast = pool.value_load(flag_sb[0:1, 0:1], min_val=0, max_val=1)
            with pool.If(fast > 0):
                with pool.Fori(0, STEPS) as s:
                    pool.wait_ge(rows_stored, s * (16 * NCH) + 16 * NLN)
                    with pool.Fori(s * NH + 1, s * NH + (NH + 1)) as h:
                        for i in range(SETS):
                            pool.wait_ge(sets_done, h * SETS + (i + 2 - SETS))
                            pool.wait_ge(idx_loaded[i], h * 16)
                            pool.sem_inc(pool_turns, 1)
                            for j in range(TS):
                                k, m = (i % RING) * TS + j, i * TS + j
                                nc.gpsimd.indirect_dma_start(
                                    G[:, k * 2 * H:(k + 1) * 2 * H], None, hrows,
                                    bass.IndirectOffsetOnAxis(ap=idx_slot[:, m:m + 1], axis=0)
                                    ).then_inc(gathered[i % RING][j], 16)

        @block.scalar
        def _(act):
            def fill_half(i, h, wait):
                if wait is not None:
                    act.wait_ge(scattered[h], wait)
                col = i * (2 * SC_HALF) + h * SC_HALF
                lo_c, hi_c = h * SC_HALF, (h + 1) * SC_HALF
                nc.scalar.copy(sc_pos[:, lo_c:hi_c], pos_i[:, bass.ds(col, SC_HALF)])
                nc.scalar.copy(sc_rec[:, lo_c:hi_c], rec[:, bass.ds(col, SC_HALF)]).then_inc(slots_filled[h], 1)

            for seg in range(len(CUTS) - 1):
                first, last = CUTS[seg] // (2 * SC_HALF), CUTS[seg + 1] // (2 * SC_HALF)
                act.wait_ge(pos_ready, seg + 1)
                if seg == 0:
                    for h in range(2):
                        fill_half(0, h, None)
                with act.Fori(max(first, 1), last) as i:
                    for h in range(2):
                        fill_half(i, h, i * (16 * SC_HALF))
            for n in range(NLN):
                act.wait_ge(var_ready, n + 1)
                nc.scalar.activation(std[:], mv[:, :, 1], ACT.Sqrt).then_inc(std_ready, 1)
            act.wait_ge(flag_ready, 1)
            fast = act.value_load(flag_sb[0:1, 0:1], min_val=0, max_val=1)
            with act.If(fast > 0):
                act.sem_inc(rows_copied, 1)
                act.sem_inc(evac_act, 3)
                with act.Fori(0, ND) as mi:
                    def one(b, tile0, units, par):
                        if par == 2:
                            act.wait_ge(stage_free[2], mi + 1)
                        else:
                            act.wait_ge(stage_free[par], mi * (DSETS // 2) + (b - par) // 2 + 1)
                        for v in range(units):
                            if v in ACT_UNITS:
                                act.wait_ge(unit_built, mi * NT + b * UNITS + (v + 1))
                                to = st_tail[:, v * CHUNK:(v + 1) * CHUNK] if par == 2 else \
                                    stage[:, par * UW + v * CHUNK:par * UW + (v + 1) * CHUNK]
                                nc.scalar.copy(to, unit_bank(v, par)[:]).then_inc(evac_act, 1)

                    build_sets(act, one)

                def scale_sum(q, bank, to):
                    act.wait_ge(agg_done, q)
                    nc.scalar.mul(to, bank[:], 1.0 / SCALE).then_inc(s_ready, 1)

                def gates(q):
                    act.wait_ge(gates_done, q)
                    act.wait_ge(h_ready, q)
                    nc.scalar.activation(r_sb, ps_r[:], ACT.Sigmoid, bias=bsum[:, 0:1])
                    nc.scalar.activation(z_sb, ps_z[:], ACT.Sigmoid, bias=bsum[:, 1:2]).then_inc(rz_ready, 1)

                def new(q):
                    act.wait_ge(t2_ready, q + 1)
                    nc.scalar.activation(n_sb[:], t_sb[:], ACT.Tanh, bias=bih_sb[:, 2:3]).then_inc(n_ready, 1)

                def rows(q, s, c):
                    act.wait_ge(rows_turned, q + 1)
                    act.wait_ge(rows_stored, q * 16 + (16 * NLN - 16))
                    nc.scalar.copy(rowbuf, ps_rows[:]).then_inc(rows_copied, 1)
                    act.wait_ge(rows_copied, q + 1)
                    at = ((s + 1) % 2) * NPAD + c * CHUNK
                    act.dma_start(hrows[bass.ds(at, CHUNK), :].rearrange("(b p) k -> p b k", p=P),
                                  rowbuf.rearrange("p (b k) -> p b k", k=2 * H)).then_inc(rows_stored, 16)

                def pair(s, mi, first):
                    q = s * NCH + mi * 2 + 2
                    gates(q - 1)
                    if not first:
                        rows(q - 2, s, mi - 1)
                    new(q - 1)
                    rows(q - 1, s, gathered_chunk(mi))
                    scale_sum(q, ps_d, S_d[:])
                    scale_sum(q + 1, ps_g, S_g)
                    gates(q)
                    new(q)

                with act.Fori(0, STEPS) as s:
                    scale_sum(s * NCH + 1, ps_g, S_g)
                    pair(s, 0, True)
                    with act.Fori(1, ND) as mi:
                        pair(s, mi, False)
                    gates(s * NCH + NCH)
                    rows(s * NCH + (NCH - 1), s, ND - 1)
                    new(s * NCH + NCH)
                    rows(s * NCH + NCH, s, NCH - 2)

        @block.tensor
        def _(pe):
            pe.wait_ge(counts_ready, 1)
            pe.matmul(ps_r[:, 0:NKEY], lhsT=ones_f, rhs=cnt[:], start=True, stop=True)
            pe.matmul(ps_z[:, 0:NKEY], lhsT=before, rhs=cnt[:], start=True, stop=True)
            for k in range(REL):
                pe.matmul(ps_in[0:NT, 0:ND], lhsT=at_win[:, k, :], rhs=cnt[:, k:ND * REL:REL], start=(k == 0), stop=(k == REL - 1))
            for k in range(REL):
                pe.matmul(ps_hn[0:NT, 0:ND], lhsT=past_win[:, k, :], rhs=cnt[:, k:ND * REL:REL], start=(k == 0), stop=(k == REL - 1))
            pe.matmul(ps_deg[:, 0:1], lhsT=after1, rhs=small[:, 0:1], start=True, stop=True).then_inc(prefix_ready, 1)
            for k in range(REL):
                mm = pe.transpose(ps_d[0:NT, k * P:(k + 1) * P], at_win[:, k, :], ident[:])
            mm.then_inc(windows_turned, 1)
            pe.wait_ge(slots_based, 1)
            for k in range(REL):
                mm = pe.matmul(ps_g[:, k * ND:(k + 1) * ND], lhsT=at_winT[0:NT, k, :], rhs=tb[0:NT, 3, :], start=True, stop=True)
            mm.then_inc(base_picked, 1)
            pe.wait_ge(bad_ready, 1)
            pe.matmul(ps_deg[:, 0:8], lhsT=ones_f, rhs=bad[:], start=True, stop=True).then_inc(bad_summed, 1)
            pe.wait_ge(weights_loaded, 16 * 10)
            for g in range(3):
                pe.transpose(ps_in[:, g * P:(g + 1) * P], wih_sb[:, g, :], ident[:])
            for g in range(3):
                mm = pe.transpose(ps_hn[:, g * P:(g + 1) * P], whh_sb[:, g, :], ident[:])
            mm.then_inc(w_turned, 1)
            pe.wait_ge(w_copied, 1)
            pe.matmul(ps_in[:, 0:3 * P], lhsT=wmsg_sb, rhs=wihT[:], start=True, stop=True)
            pe.matmul(ps_hn[0:1, 0:3 * P], lhsT=bmsg_sb[:, 0:1], rhs=wihT[:], start=True, stop=True).then_inc(w_turned, 1)
            pe.sem_inc(hot_used, 2)
            pe.matmul(ps_r[0:NW, 0:P], lhsT=zeros_h[0:1, 0:NW], rhs=zeros_h[:, 0:P], start=True, stop=False)
            with pe.Fori(0, K // (2 * HB)) as i:
                for a in range(2):
                    pe.wait_ge(hot_ready, i * 2 + (a + 1))
                    for v in range(HB):
                        mm = pe.matmul(ps_r[0:NW, 0:P], lhsT=hot_w[a][:, v * P:v * P + NW], rhs=hot_l[a][:, v * P:(v + 1) * P],
                                       start=False, stop=False)
                    mm.then_inc(hot_used, 1)
            pe.matmul(ps_r[0:NW, 0:P], lhsT=zeros_h[0:1, 0:NW], rhs=zeros_h[:, 0:P], start=False, stop=True).then_inc(hot_used, 1)
            for g in range(NLN):
                pe.wait_ge(ln_rows_ready, g + 1)
                for t in range(LNT):
                    n = g * LNT + t
                    if n >= 2:
                        pe.wait_ge(lnT_copied, n - 1)
                    pe.transpose((ps_d, ps_g)[n % 2][:, 0:P], xg[:, g % 2, t, :], ident[:]).then_inc(lnT_ready, 1)
            pe.wait_ge(lnT_copied, NT)
            pe.wait_ge(w_copied, 4)
            pe.wait_ge(tables_ready, 1)
            pe.wait_ge(c9_loaded, 16)
            fast = pe.value_load(flag_sb[0:1, 0:1], min_val=0, max_val=1)
            with pe.If(fast > 0):
                pe.sem_inc(sets_done, 4)
                pe.sem_inc(dense_done, 1)
                pe.sem_inc(tails_done, 1)
                pe.sem_inc(rows_turned, 1)
                with pe.Fori(0, ND) as mi:
                    def one(b, tile0, units, par):
                        slot0 = (par % 2) * 12 if par != 2 else 0
                        pe.wait_ge(set_hot, mi * (DSETS + 1) + b + 1)
                        for v in range(units):
                            if v in ACT_UNITS:
                                pe.wait_ge(evac_act, mi * ACT_CHUNK + b * len(ACT_UNITS) + (v + 1))
                            else:
                                pe.wait_ge(evac_dve, mi * DVE_CHUNK + b + 1)
                            tiles = unit_tiles(b, v)
                            for n, t in enumerate(tiles):
                                k = slot0 + t
                                mm = pe.matmul(unit_bank(v, par)[:], lhsT=ohd[:, k * P:(k + 1) * P], rhs=ohs[:, k * CHUNK:(k + 1) * CHUNK],
                                               start=(n == 0), stop=(n == len(tiles) - 1))
                            mm.then_inc(unit_built, 1)

                    build_sets(pe, one)

                def open_bank(bank):
                    pe.matmul(bank[:], lhsT=zeros_h[0:1, 0:P], rhs=zeros_h[:], start=True, stop=False)

                def close_bank(bank):
                    return pe.matmul(bank[:], lhsT=zeros_h[0:1, 0:P], rhs=zeros_h[:], start=False, stop=True)

                def dense_unit(mi, slot, v, u):
                    j = (mi * OWN + u) % NT
                    blk = a_ring[:, slot * UW + v * CHUNK:slot * UW + (v + 1) * CHUNK] if slot is not None else \
                        a_tail[:, v * CHUNK:(v + 1) * CHUNK]
                    at = j * (2 * H)
                    if not isinstance(at, int):
                        at = at.with_bounds(max_val=(NT - 1) * 2 * H)
                    pe.matmul(ps_d[:], lhsT=hr[:, bass.ds(at, H)], rhs=blk, start=False, stop=False)
                    return pe.matmul(ps_d[:], lhsT=hr[:, bass.ds(at + H, H)], rhs=blk, start=False, stop=False)

                def gather_tile(h, i, j, half):
                    k = (i % RING) * TS + j
                    yield_to = ps_g[:, half * HALF:(half + 1) * HALF]
                    pe.wait_ge(gathered[i % RING][j], h)
                    pe.matmul(yield_to, lhsT=G[:, k * 2 * H:k * 2 * H + H], rhs=OH[:, k * HALF:(k + 1) * HALF], start=False, stop=False)
                    return pe.matmul(yield_to, lhsT=G[:, k * 2 * H + H:(k + 1) * 2 * H], rhs=OH[:, k * HALF:(k + 1) * HALF],
                                     start=False, stop=False)

                def gates(q, S, d9, loads, c):
                    pe.wait_ge(s_ready, q)
                    pe.wait_ge(deg9_loaded[d9], loads)
                    pe.wait_ge(rz_ready, q)
                    pe.wait_ge(t2_ready, q)
                    h_c, d_c = hT[:, bass.ds(c * CHUNK, CHUNK)], deg9[d9][:]
                    for g, bank in ((0, ps_r), (1, ps_z)):
                        w = slice(g * P, (g + 1) * P)
                        pe.matmul(bank[:], lhsT=wfT[:, w], rhs=S, start=True, stop=False)
                        pe.matmul(bank[:], lhsT=whhT[:, w], rhs=h_c, start=False, stop=False)
                        pe.matmul(bank[:], lhsT=c9[:, w], rhs=d_c, start=False, stop=True)
                    w = slice(2 * P, 3 * P)
                    pe.matmul(ps_hn[:], lhsT=whhT[:, w], rhs=h_c, start=True, stop=True)
                    pe.matmul(ps_in[:], lhsT=wfT[:, w], rhs=S, start=True, stop=False)
                    pe.matmul(ps_in[:], lhsT=c9[:, w], rhs=d_c, start=False, stop=True).then_inc(gates_done, 1)

                def turn(q):
                    pe.wait_ge(h_ready, q + 1)
                    pe.wait_ge(rows_copied, q)
                    for b in range(4):
                        for a, part in enumerate((hi, lo)):
                            mm = pe.transpose(ps_rows[:, (2 * b + a) * P:(2 * b + a + 1) * P], part[:, b * P:(b + 1) * P], ident_h[:])
                    mm.then_inc(rows_turned, 1)

                pe.wait_ge(evac_act, ND * ACT_CHUNK + 3)
                pe.wait_ge(evac_dve, ND * DVE_CHUNK + 1)
                pe.sem_inc(rz_ready, 1)
                pe.sem_inc(t2_ready, 1)

                def pair(s, mi, first):
                    q = s * NCH + mi * 2 + 2
                    open_bank(ps_d)
                    pe.wait_ge(s_ready, q - 1)
                    open_bank(ps_g)
                    for half in range(2):
                        h = s * NH + mi * 2 + (half + 2)
                        for i in range(SETS):
                            a3 = s * (ND * DSETS // RING) + mi * (DSETS // RING) + (half * SETS + i) // RING
                            pe.wait_ge(oh_ready, h * SETS + (i - SETS + 1))
                            pe.wait_ge(a_loaded[i % RING], a3 * 16 + 16)
                            for v in range(UNITS):
                                du = dense_unit(mi, i % RING, v, (half * SETS + i) * UNITS + v)
                                if v == UNITS - 1:
                                    du.then_inc(dense_done, 1)
                                if v < TS:
                                    mm = gather_tile(h * 32 + (16 * (i // RING + 1) - 32), i, v, half)
                                    if v == TS - 1:
                                        mm.then_inc(sets_done, 1)
                            if half == 0 and i == 0:
                                gates(q - 1, S_g, 1, s * (16 * (ND + 1)) + mi * 16 + 16, gathered_chunk(mi))
                                if not first:
                                    turn(q - 2)
                            if half == 0 and i == 2:
                                turn(q - 1)
                    pe.wait_ge(tail_loaded, s * (16 * ND) + mi * 16 + 16)
                    for v in range(TAIL):
                        mm = dense_unit(mi, None, v, DSETS * UNITS + v)
                    mm.then_inc(tails_done, 1)
                    close_bank(ps_d).then_inc(agg_done, 1)
                    close_bank(ps_g).then_inc(agg_done, 1)
                    gates(q, S_d[:], 0, s * (16 * ND) + mi * 16 + 16, mi)

                with pe.Fori(0, STEPS) as s:
                    h0 = s * NH + 1
                    open_bank(ps_g)
                    for i in range(SETS):
                        pe.wait_ge(oh_ready, h0 * SETS + (i - SETS + 1))
                        for j in range(TS):
                            mm = gather_tile(h0 * 32 + (16 * (i // RING + 1) - 32), i, j, 0)
                        mm.then_inc(sets_done, 1)
                    close_bank(ps_g).then_inc(agg_done, 1)
                    pe.wait_ge(rows_loaded, s * (16 * NLN) + 16 * NLN)
                    pe.sem_inc(pe_turns, 1)
                    pair(s, 0, True)
                    with pe.Fori(1, ND) as mi:
                        pair(s, mi, False)
                    gates(s * NCH + NCH, S_g, 1, s * (16 * (ND + 1)) + 16 * (ND + 1), NCH - 2)
                    turn(s * NCH + (NCH - 1))
                    turn(s * NCH + NCH)

        @block.vector
        def _(dve):
            done = [0]

            def link(ins):
                done[0] += 1
                ins.then_inc(dve_step, 1)
                dve.wait_ge(dve_step, done[0])

            nc.vector.memset(src_sb[96:P, REM:K], PAD_NODE).then_inc(edges_padded, 1)
            nc.vector.memset(dst_sb[96:P, REM:K], N - 1).then_inc(edges_padded, 1)
            nc.vector.memset(rec_sb[:], NO_NODE).then_inc(fill_ready, 1)
            nc.vector.memset(hT[:], 0.0).then_inc(zeros_ready, 1)
            nc.vector.memset(ones_f, 1.0)
            nc.vector.memset(zeros_h[:], 0.0)
            nc.vector.memset(bad[:], 0.0)
            nc.vector.memset(pos, 0.0)
            dve.wait_ge(iota_done, 2)
            nc.vector.tensor_copy(iota_h[:], iota_i[:])
            nc.vector.tensor_copy(iota_b[:], iota_i[:, 0:P])
            link(nc.vector.tensor_copy(part_f[:], part_i[:]))
            link(nc.vector.tensor_copy(iota_f[:], iota_i[:, 0:P]))
            nc.vector.tensor_scalar(ident[:], iota_f[:], part_f[:, 0:1], None, ALU.is_equal)
            nc.vector.tensor_scalar(ident_h[:], iota_f[:], part_f[:, 0:1], None, ALU.is_equal)
            nc.vector.tensor_scalar(after1, iota_f[:], 1.0, part_f[:, 0:1], ALU.add, ALU.is_equal)
            nc.vector.tensor_scalar(before, iota_f[:], part_f[:, 0:1], None, ALU.is_gt)
            link(nc.vector.tensor_scalar(tb[:, 0, :], iota_f[:, 0:ND], -float(OWN), part_f[:, 0:1], ALU.mult, ALU.add))
            link(nc.vector.tensor_scalar(tb[:, 1, :], tb[:, 0, :], 0.0, float(NT), ALU.is_lt, ALU.mult))
            link(nc.vector.tensor_tensor(tb[:, 0, :], tb[:, 0, :], tb[:, 1, :], ALU.add))
            link(nc.vector.tensor_scalar(tb[:, 1, :], tb[:, 0, :], float(OWN), float(P), ALU.is_lt, ALU.mult))
            link(nc.vector.tensor_scalar(tb[:, 1, :], tb[:, 1, :], float(P), None, ALU.add))
            link(nc.vector.tensor_scalar(tb[:, 2, :], tb[:, 0, :], float(OWN), None, ALU.min))
            link(nc.vector.tensor_tensor(tb[:, 2, :], tb[:, 2, :], tb[:, 0, :], ALU.add))
            link(nc.vector.scalar_tensor_tensor(out=tb[:, 2, :], in0=iota_f[:, 0:ND], scalar=float(DT), in1=tb[:, 2, :],
                                                op0=ALU.mult, op1=ALU.add))
            link(nc.vector.tensor_scalar(tb[:, 2, :], tb[:, 2, :], float(P), None, ALU.mult))
            dve.wait_ge(edges_loaded, 64)
            link(nc.vector.tensor_scalar(tmp_i, dst_sb, 7, None, ALU.logical_shift_right))
            link(nc.vector.tensor_copy(small[:, 0:1], tmp_i[:, 0:1]))
            nc.vector.tensor_copy(small[:, 1:2], tmp_i[:, K - 1:K])
            link(nc.vector.tensor_tensor(tmp_f[:, 0:K - 1], tmp_i[:, 0:K - 1], tmp_i[:, 1:K], ALU.subtract))
            link(nc.vector.tensor_reduce(bad[:, 0:1], tmp_f[:, 0:K - 1], AX_X, ALU.max))
            link(nc.vector.tensor_scalar(tmp_f, tmp_i, small[:, 0:1], None, ALU.subtract))
            link(nc.vector.tensor_scalar(bad[:, 1:2], small[:, 1:2], small[:, 0:1], -float(REL - 1), ALU.subtract, ALU.add))
            link(nc.vector.tensor_scalar(tmp_i, src_sb, 9, None, ALU.logical_shift_right))
            link(nc.vector.tensor_scalar(pos_i, src_sb, 8, None, ALU.logical_shift_right))
            link(nc.vector.tensor_scalar(pos, pos_i, float((REL - 2) * ND), None, ALU.add))
            link(nc.vector.scalar_tensor_tensor(out=tmp_f, in0=tmp_i, scalar=float(REL), in1=tmp_f, op0=ALU.mult, op1=ALU.add))
            link(nc.vector.tensor_tensor(tmp_f, tmp_f, pos, ALU.subtract))
            link(nc.vector.scalar_tensor_tensor(out=tmp_f, in0=tmp_i, scalar=float(ND), in1=tmp_f, op0=ALU.is_lt, op1=ALU.mult))
            link(nc.vector.tensor_tensor(key_b, tmp_f, pos, ALU.add))
            link(nc.vector.tensor_scalar(tmp_i, src_sb, CHUNK - 1, None, ALU.bitwise_and))
            link(nc.vector.scalar_tensor_tensor(out=rec, in0=dst_sb, scalar=10, in1=tmp_i, op0=ALU.logical_shift_left, op1=ALU.bitwise_or))
            link(nc.vector.tensor_scalar(tmp_i, src_sb, 7, None, ALU.logical_shift_right))
            link(nc.vector.tensor_copy(win_f, tmp_i))
            link(nc.vector.tensor_scalar(tmp_i, src_sb, P - 1, None, ALU.bitwise_and))
            link(nc.vector.tensor_copy(loc_f, tmp_i))
            for k in range(REL):
                link(nc.vector.tensor_scalar(small[:, 2 + k:3 + k], small[:, 0:1], float(k), None, ALU.add))
                nc.vector.tensor_scalar(at_win[:, k, :], iota_f[:, 0:NT], small[:, 2 + k:3 + k], None, ALU.is_equal)
                link(nc.vector.tensor_scalar(past_win[:, k, :], iota_f[:, 0:NT], small[:, 2 + k:3 + k], None, ALU.is_gt))
            with dve.Fori(1, NKEY + 1) as b:
                nc.vector.tensor_scalar(mask, key_b, iota_f[:, bass.ds(b - 1, 1)], 0.0, ALU.is_equal, ALU.add,
                                        accum_out=cnt[:, bass.ds(b - 1, 1)]).then_inc(keys_counted, 1)
                dve.wait_ge(keys_counted, b)
            dve.drain().then_inc(counts_ready, 1)
            dve.wait_ge(windows_turned, 1)
            for k in range(REL):
                last = nc.vector.tensor_copy(at_winT[0:NT, k, :], ps_d[0:NT, k * P:(k + 1) * P])
            link(last)
            dve.wait_ge(prefix_ready, 1)
            link(nc.vector.tensor_tensor(tb[0:NT, 3, :], tb[0:NT, 2, :], ps_hn[0:NT, 0:ND], ALU.subtract))
            dve.drain().then_inc(slots_based, 1)
            pre = base[:, 0:ND * REL].rearrange("p (c k) -> p c k", k=REL)
            nc.vector.tensor_copy(base[:], ps_z[:, 0:NKEY])
            link(nc.vector.tensor_tensor(tb[0:NT, 1, :], ps_in[0:NT, 0:ND], tb[0:NT, 1, :], ALU.subtract))
            link(nc.vector.tensor_reduce(bad[0:NT, 2:3], tb[0:NT, 1, :], AX_X, ALU.max))
            link(nc.vector.tensor_reduce(bad[:, 3:4], ps_r[:, ND * REL:NKEY], AX_X, ALU.max))
            link(nc.vector.tensor_scalar(bad[:, 3:4], bad[:, 3:4], -float(HT * P), None, ALU.add))
            link(nc.vector.tensor_tensor(bad[:, 4:5], small[:, 1:2], ps_deg[:, 0:1], ALU.subtract))
            link(nc.vector.tensor_scalar(small[:, 6:7], part_f[:], float(P - 1), None, ALU.is_lt))
            link(nc.vector.tensor_tensor(bad[:, 4:5], bad[:, 4:5], small[:, 6:7], ALU.mult))
            link(nc.vector.tensor_scalar(bad[:], bad[:], 0.0, None, ALU.max))
            dve.drain().then_inc(bad_ready, 1)
            link(nc.vector.tensor_reduce(tb[:, 1, :], pre, AX_X, ALU.add))
            cnt3 = cnt[:, 0:ND * REL].rearrange("p (c k) -> p c k", k=REL)
            dve.wait_ge(base_picked, 1)
            for k in range(REL):
                link(nc.vector.tensor_tensor(pre[:, :, k], ps_g[:, k * ND:(k + 1) * ND], tb[:, 1, :], ALU.add))
                if k < REL - 1:
                    link(nc.vector.tensor_tensor(tb[:, 1, :], tb[:, 1, :], cnt3[:, :, k], ALU.add))
            halves = base[:, ND * REL:NKEY]
            link(nc.vector.scalar_tensor_tensor(out=halves, in0=iota_f[:, 0:NH], scalar=float(HT * P), in1=halves, op0=ALU.mult, op1=ALU.add))
            link(nc.vector.tensor_scalar(halves, halves, float(G0 * P), None, ALU.add))
            dve.wait_ge(bad_summed, 1)
            link(nc.vector.tensor_reduce(small[:, 7:8], ps_deg[:, 0:8], AX_X, ALU.add))
            nc.vector.tensor_scalar(flag_sb[0:1, :], small[0:1, 7:8], 0.0, None, ALU.is_le).then_inc(flag_ready, 1)
            for seg in range(len(CUTS) - 1):
                cols = slice(CUTS[seg], CUTS[seg + 1])
                with dve.Fori(seg * NKEY + 1, (seg + 1) * NKEY + 1) as b:
                    key = b - (seg * NKEY + 1)
                    nc.vector.tensor_scalar(mask[:, cols], key_b[:, cols], iota_f[:, bass.ds(key, 1)], None, ALU.is_equal).then_inc(key_masked, 1)
                    dve.wait_ge(key_masked, b)
                    nc.vector.tensor_tensor_scan(tmp_f[:, cols], mask[:, cols], mask[:, cols], base[:, bass.ds(key, 1)],
                                                 ALU.add, ALU.max).then_inc(key_ranked, 1)
                    dve.wait_ge(iota_done, 2)
                    dve.wait_ge(key_ranked, b)
                    nc.vector.copy_predicated(pos[:, cols], mask[:, cols], tmp_f[:, cols]).then_inc(key_placed, 1)
                    nc.vector.tensor_scalar(base[:, bass.ds(key, 1)], tmp_f[:, CUTS[seg + 1] - 1:CUTS[seg + 1]], 0.0, None,
                                            ALU.add).then_inc(key_carried, 1)
                    dve.wait_ge(key_placed, b)
                    dve.wait_ge(key_carried, b)
                link(nc.vector.tensor_scalar(pos[:, cols], pos[:, cols], -1.0, 0.0, ALU.add, ALU.max))
                link(nc.vector.tensor_scalar(pos_i[:, cols], pos[:, cols], float(P * T - 1), None, ALU.min))
                link(nc.vector.tensor_scalar(tmp_i[:, cols], pos_i[:, cols], 7, None, ALU.logical_shift_right))
                link(nc.vector.tensor_scalar(pos_i[:, cols], pos_i[:, cols], P - 1, None, ALU.bitwise_and))
                link(nc.vector.scalar_tensor_tensor(out=pos[:, cols], in0=pos_i[:, cols], scalar=float(T), in1=tmp_i[:, cols],
                                                    op0=ALU.mult, op1=ALU.add))
                link(nc.vector.tensor_copy(pos_i[:, cols], pos[:, cols]))
                dve.sem_inc(pos_ready, 1)
            dve.wait_ge(w_turned, 1)
            nc.vector.tensor_copy(wihT[:], ps_in[:, 0:3 * P])
            nc.vector.tensor_copy(whhT[:], ps_hn[:, 0:3 * P]).then_inc(w_copied, 1)
            dve.wait_ge(w_turned, 2)
            nc.vector.tensor_copy(wfT[:], ps_in[:, 0:3 * P]).then_inc(w_copied, 1)
            link(nc.vector.tensor_copy(cdeg, ps_hn[0:1, 0:3 * P]))
            nc.vector.tensor_tensor(bsum[:], bih_sb[:], bhh_sb[:], ALU.add).then_inc(w_copied, 1)
            for a in range(3):
                link(nc.vector.tensor_copy(cpart[:, a, :], cdeg))
                if a < 2:
                    link(nc.vector.tensor_tensor(cdeg, cdeg, cpart[:, a, :], ALU.subtract))
            dve.drain().then_inc(c_parts, 1)
            with dve.Fori(0, K // (2 * HB)) as i:
                for a in range(2):
                    dve.wait_ge(hot_used, i * 2 + (a + 1))
                    for v in range(HB):
                        col = i * (2 * HB) + (a * HB + v)
                        nc.vector.tensor_scalar(hot_l[a][:, v * P:(v + 1) * P], iota_b[:], loc_f[:, bass.ds(col, 1)], None, ALU.is_equal)
                        ins = nc.vector.tensor_scalar(hot_w[a][:, v * P:(v + 1) * P], iota_b[:], win_f[:, bass.ds(col, 1)], None, ALU.is_equal)
                    ins.then_inc(hot_ready, 1)
            dve.wait_ge(hot_used, K // HB + 3)
            link(nc.vector.tensor_copy(deg_f[0:NW, 0:P], ps_r[0:NW, 0:P]))
            for b in range(3):
                part = dpart[0:NW, b * P:(b + 1) * P]
                link(nc.vector.tensor_copy(part, deg_f[0:NW, 0:P]))
                if b < 2:
                    link(nc.vector.tensor_tensor(deg_f[0:NW, 0:P], deg_f[0:NW, 0:P], part, ALU.subtract))
            dve.drain().then_inc(deg_parts, 1)
            loaded = [0, 0]
            for g in range(NLN):
                loaded[g % 2] += 16 * PIECES[g]
                xt = xg[:, g % 2]
                dve.wait_ge(x_loaded[g % 2], loaded[g % 2])
                for t in range(LNT):
                    link(nc.vector.bn_stats(stats[:], xt[:, t, :]))
                    link(nc.vector.bn_aggr(mv[:, t, :], stats[:]))
                link(nc.vector.tensor_scalar(mv[:, :, 1], mv[:, :, 1], EPS, None, ALU.add))
                dve.sem_inc(var_ready, 1)
                dve.wait_ge(std_ready, g + 1)
                link(nc.vector.reciprocal(rstd[:], std[:]))
                for t in range(LNT):
                    last = nc.vector.tensor_scalar(xt[:, t, :], xt[:, t, :], mv[:, t, 0:1], rstd[:, t:t + 1], ALU.subtract, ALU.mult)
                link(last)
                link(nc.vector.tensor_scalar(xt, xt, 0.0, None, ALU.max))
                if g >= 1:
                    dve.wait_ge(rows_stored, 16 * g)
                link(nc.vector.tensor_scalar(lnrow[:, :, 0, :], xt, SCALE, None, ALU.mult))
                nc.vector.scalar_tensor_tensor(out=lnrow[:, :, 1, :], in0=xt, scalar=SCALE, in1=lnrow[:, :, 0, :],
                                               op0=ALU.mult, op1=ALU.subtract).then_inc(ln_rows_ready, 1)
                dve.wait_ge(zeros_stored, 32)
                for t in range(LNT):
                    n = g * LNT + t
                    dve.wait_ge(lnT_ready, n + 1)
                    nc.vector.tensor_copy(hT[:, n * P:(n + 1) * P], (ps_d, ps_g)[n % 2][:, 0:P]).then_inc(lnT_copied, 1)
            dve.sem_inc(w_copied, 1)
            dve.wait_ge(rec_loaded, 16)
            link(nc.vector.tensor_scalar(pos_i[:, 0:G0], rec_sb[:, 0:G0], 10, P - 1, ALU.logical_shift_right, ALU.bitwise_and))
            link(nc.vector.tensor_scalar(idx_tab[:, 0:NH * HT], rec_sb[:, G0:T], 10, None, ALU.logical_shift_right))
            link(nc.vector.tensor_scalar(rec_sb[:], rec_sb[:], NO_NODE, None, ALU.bitwise_and))
            nc.vector.tensor_copy(loc_d, rec_sb[:, 0:G0])
            nc.vector.tensor_copy(dst_d, pos_i[:, 0:G0])
            nc.vector.tensor_copy(loc_g[:], rec_sb[:, G0:T])
            link(nc.vector.tensor_scalar(idx_tab[:, NH * HT:2 * NH * HT], idx_tab[:, 0:NH * HT], float(NPAD), None, ALU.add))
            dve.drain().then_inc(tables_ready, 1)
            fast = dve.value_load(flag_sb[0:1, 0:1], min_val=0, max_val=1)
            with dve.If(fast > 0):
                dve.sem_inc(h_ready, 1)
                dve.sem_inc(evac_dve, 1)
                for par in range(3):
                    dve.sem_inc(stage_free[par], 1)
                with dve.Fori(0, ND) as mi:
                    def hots(b, tile0, units, par):
                        slot0 = (par % 2) * 12
                        for v in range(units):
                            for t in unit_tiles(b, v):
                                k = slot0 + t
                                col = (mi * DT + tile0 + t).with_bounds(max_val=G0 - 1)
                                nc.vector.tensor_scalar(ohs[:, k * CHUNK:(k + 1) * CHUNK], iota_h[:], loc_d[:, bass.ds(col, 1)], None, ALU.is_equal)
                                ins = nc.vector.tensor_scalar(ohd[:, k * P:(k + 1) * P], iota_h[:, 0:P], dst_d[:, bass.ds(col, 1)], None, ALU.is_equal)
                        ins.then_inc(set_hot, 1)

                    def evac(b, par):
                        dve.wait_ge(stage_free[par], mi * (DSETS // 2) + (b - par) // 2 + 1)
                        for v in range(UNITS):
                            if v not in ACT_UNITS:
                                dve.wait_ge(unit_built, mi * NT + b * UNITS + (v + 1))
                                nc.vector.tensor_copy(stage[:, par * UW + v * CHUNK:par * UW + (v + 1) * CHUNK],
                                                      unit_bank(v, par)[:]).then_inc(evac_dve, 1)

                    hots(0, 0, UNITS, 0)
                    with dve.Fori(0, (DSETS - 2) // 2) as bb:
                        hots(bb * 2 + 1, bb * (2 * UNITS) + UNITS + OWN, UNITS, 1)
                        evac(bb * 2, 0)
                        hots(bb * 2 + 2, bb * (2 * UNITS) + 2 * UNITS + OWN, UNITS, 0)
                        evac(bb * 2 + 1, 1)
                    hots(DSETS - 1, (DSETS - 1) * UNITS + OWN, UNITS, 1)
                    evac(DSETS - 2, 0)
                    hots(DSETS, DSETS * UNITS + OWN, TAIL, 2)
                    evac(DSETS - 1, 1)
                    dve.wait_ge(unit_built, mi * NT + NT)

                def set_hots(h, i, half):
                    n = h * SETS + (i - SETS + 1)
                    dve.wait_ge(sets_done, n + 1)
                    for j in range(TS):
                        k = (i % RING) * TS + j
                        col = ((h + (NH - 2)) % NH) * HT + (i * TS + j)
                        ins = nc.vector.tensor_scalar(OH[:, k * HALF:(k + 1) * HALF], iota_h[:, half * HALF:(half + 1) * HALF],
                                                      loc_g[:, bass.ds(col, 1)], None, ALU.is_equal)
                    ins.then_inc(oh_ready, 1)

                def update(q, c):
                    h_c = hT[:, bass.ds(c * CHUNK, CHUNK)]
                    dve.wait_ge(rz_ready, q + 1)
                    nc.vector.scalar_tensor_tensor(out=t_sb[:], in0=ps_hn[:], scalar=bhh_sb[:, 2:3], in1=r_sb,
                                                   op0=ALU.add, op1=ALU.mult).then_inc(t_done, 1)
                    dve.wait_ge(t_done, q)
                    nc.vector.tensor_tensor(t_sb[:], ps_in[:], t_sb[:], ALU.add).then_inc(t2_ready, 1)
                    dve.wait_ge(n_ready, q)
                    nc.vector.tensor_tensor(t_sb[:], h_c, n_sb[:], ALU.subtract).then_inc(upd_step, 1)
                    dve.wait_ge(upd_step, q * 4 - 3)
                    nc.vector.tensor_tensor(t_sb[:], t_sb[:], z_sb, ALU.mult).then_inc(upd_step, 1)
                    dve.wait_ge(upd_step, q * 4 - 2)
                    nc.vector.tensor_tensor(h_c, n_sb[:], t_sb[:], ALU.add).then_inc(upd_step, 1)
                    dve.wait_ge(upd_step, q * 4 - 1)
                    dve.wait_ge(rows_turned, q)
                    nc.vector.tensor_scalar(hi[:], h_c, SCALE, None, ALU.mult).then_inc(upd_step, 1)
                    dve.wait_ge(upd_step, q * 4)
                    nc.vector.scalar_tensor_tensor(out=lo[:], in0=h_c, scalar=SCALE, in1=hi[:],
                                                   op0=ALU.mult, op1=ALU.subtract).then_inc(h_ready, 1)

                def pair(s, mi, first):
                    q = s * NCH + mi * 2 + 2
                    h = s * NH + mi * 2 + 2
                    if not first:
                        update(q - 2, mi - 1)
                    set_hots(h, RING, 0)
                    update(q - 1, gathered_chunk(mi))
                    for i in range(RING + 1, SETS):
                        set_hots(h, i, 0)
                    for i in range(SETS):
                        set_hots(h + 1, i, 1)
                    for i in range(RING):
                        set_hots(h + 2, i, 0)

                for i in range(RING):
                    set_hots(1, i, 0)
                with dve.Fori(0, STEPS) as s:
                    for i in range(RING, SETS):
                        set_hots(s * NH + 1, i, 0)
                    for i in range(RING):
                        set_hots(s * NH + 2, i, 0)
                    pair(s, 0, True)
                    with dve.Fori(1, ND) as mi:
                        pair(s, mi, False)
                    update(s * NCH + (NCH - 1), ND - 1)
                    update(s * NCH + NCH, NCH - 2)
                loaded = [0, 0]
                for g in range(NLN):
                    loaded[g % 2] += 16 * (1 + PIECES[g])
                    dve.wait_ge(fin_rows[g % 2], loaded[g % 2])
                    rows, xt = fin_bufs(g % 2), xg[:, g % 2]
                    for part in range(2):
                        ins = nc.vector.scalar_tensor_tensor(out=xt, in0=rows[:, :, part * H:(part + 1) * H], scalar=1.0 / SCALE,
                                                             in1=xt, op0=ALU.mult, op1=ALU.add)
                        if part == 0:
                            link(ins)
                    ins.then_inc(fin_ready, 1)

    return steps_only


def build_general(nc, ctx, steps_only, verdict, x, src, dst, W_msg, b_msg, W_ih, W_hh, b_ih, b_hh, out):
    N, H = x.shape
    E = src.shape[0]
    assert H == P
    NCH = -(-N // CHUNK)
    NPAD = NCH * CHUNK
    NT = -(-N // P)
    K = -(-E // (P * 2 * SC_HALF)) * 2 * SC_HALF
    FULL = E // K
    REM = E - FULL * K
    assert FULL == P - 1
    GE = GROUP * P
    GMAX = -(-((P * K) // GE + NCH) // ISETS) * ISETS
    T = GMAX * GROUP
    LNT = 14
    assert NT % LNT == 0
    NLN = NT // LNT
    NFULL = N // P
    NREM = N - NFULL * P

    rec_dram = nc.dram_tensor("rec_dram", (P * T, 1), I32, kind="Internal").ap()
    hrows = nc.dram_tensor("hrows", (2 * NPAD, 2 * H), F16, kind="Internal").ap()

    with ExitStack() as mem:
        def sb(name, shape, dt):
            return mem.enter_context(nc.sbuf_tensor(name, shape, dt))

        def psum(name, shape, dt):
            return mem.enter_context(nc.psum_tensor(name, shape, dt))

        def sem(name):
            return steps_only[name] if name in steps_only else ctx.enter_context(nc.semaphore(name))

        ps_agg = psum("ps_agg", [P, 2 * CHUNK], F32)
        ps_r = psum("ps_r", [P, CHUNK], F32)
        ps_z = psum("ps_z", [P, CHUNK], F32)
        ps_in = psum("ps_in", [P, CHUNK], F32)
        ps_hn = psum("ps_hn", [P, CHUNK], F32)
        ps_rows = psum("ps_rows", [P, 8 * P], F16)
        ps_deg = psum("ps_deg", [P, CHUNK], F32)

        early = sb("early", [P, 4 * K], I32)
        src_sb = early[:, 0:K]
        dst_sb = early[:, K:2 * K]
        chunk_i = early[:, 2 * K:3 * K]
        scan = early[:, 3 * K:4 * K].bitcast(F32)
        idx_tab = early[:, 0:2 * T]
        loc_tab = early[:, 2 * T:3 * T].bitcast(F32)
        mid = sb("mid", [P, 3 * K], I32)
        pos = mid[:, 0:K].bitcast(F32)
        pos_i = mid[:, K:2 * K]
        rec = mid[:, 2 * K:3 * K]
        pos_hi = chunk_i
        chunk_b = sb("chunk_b", [P, K], BF16)
        mask = sb("mask", [P, K], U16)
        rec_sb = sb("rec_sb", [P, T], I32)
        fill = rec_sb
        sc_pos = sb("sc_pos", [P, 2 * SC_HALF], I32)
        sc_rec = sb("sc_rec", [P, 2 * SC_HALF], I32)

        iota_i = sb("iota_i", [P, CHUNK], I32)
        iota_h = sb("iota_h", [P, CHUNK], F16)
        iota_f = sb("iota_f", [P, P], F32)
        part_i = sb("part_i", [P, 1], I32)
        part_f = sb("part_f", [P, 1], F32)
        ident = sb("ident", [P, P], F32)
        ident_h = sb("ident_h", [P, P], F16)
        before = sb("before", [P, P], F32)
        ones_f = sb("ones_f", [P, P], F32)
        ones_h = sb("ones_h", [P, 1], F16)
        zeros_h = sb("zeros_h", [1, CHUNK], F16)
        cnt = sb("cnt", [P, NCH], F32)
        base = sb("base", [P, NCH], F32)
        grp_i = sb("grp_i", [P, NCH], I32)
        grp_f = sb("grp_f", [P, NCH], F32)
        cum = sb("cum", [P, 2, NCH], F32)
        start_f = sb("start_f", [P, NCH], F32)
        chunk_end = sb("chunk_end", [P, NCH + 1], I32)

        wmsg_sb = sb("wmsg_sb", [P, P], F32)
        wih_sb = sb("wih_sb", [P, 3, P], F32)
        whh_sb = sb("whh_sb", [P, 3, P], F32)
        wihT = sb("wihT", [P, 3 * P], F32)
        whhT = sb("whhT", [P, 3 * P], F32)
        wfT = sb("wfT", [P, 3 * P], F32)
        cdeg = sb("cdeg", [1, 3 * P], F32)
        bmsg_sb = sb("bmsg_sb", [P, 1], F32)
        bih_sb = sb("bih_sb", [P, 3], F32)
        bhh_sb = sb("bhh_sb", [P, 3], F32)
        bsum = sb("bsum", [P, 3], F32)

        hT = sb("hT", [P, NPAD], F32)
        deg = sb("deg", [1, NPAD], F32)
        xg = sb("xg", [P, 2, LNT, P], F32)
        stats = sb("stats", [P, 6], F32)
        mv = sb("mv", [P, LNT, 2], F32)
        std = sb("std", [P, LNT], F32)
        rstd = sb("rstd", [P, LNT], F32)
        lnrow = sb("lnrow", [P, LNT, 2, P], F16)

        idx_slot = sb("idx_slot", [P, ISETS * GROUP], I32)
        G = sb("G", [P, 2 * GROUP * 2 * H], F16)
        OH = mid[:, 0:OHR * CHUNK // 2].bitcast(F16)
        srz = lnrow[:].rearrange("p t a k -> p (t a k)").bitcast(F32)
        S = srz[:, 0:CHUNK]
        r_sb = srz[:, CHUNK:2 * CHUNK]
        z_sb = srz[:, 2 * CHUNK:3 * CHUNK]
        t_sb = sb("t_sb", [P, CHUNK], F32)
        n_sb = sb("n_sb", [P, CHUNK], F32)
        hi = sb("hi", [P, CHUNK], F16)
        lo = sb("lo", [P, CHUNK], F16)
        rowbuf = iota_i[:].bitcast(F16)

        edges_padded = sem("edges_padded")
        edges_loaded = sem("edges_loaded")
        fill_ready = sem("fill_ready")
        zeros_ready = sem("zeros_ready")
        zeros_stored = sem("zeros_stored")
        rec_filled = sem("rec_filled")
        weights_loaded = sem("weights_loaded")
        iota_done = sem("iota_done")
        consts_ready = sem("consts_ready")
        dve_step = sem("dve_step")
        counts_ready = sem("counts_ready")
        prefix_ready = sem("prefix_ready")
        mask_step = sem("mask_step")
        rank_step = sem("rank_step")
        chunk_masked = sem("chunk_masked")
        chunk_ranked = sem("chunk_ranked")
        chunk_placed = sem("chunk_placed")
        pos_cleared = sem("pos_cleared")
        pos_ready = sem("pos_ready")
        slots_filled = [sem("slots_filled_0"), sem("slots_filled_1")]
        scattered = [sem("scattered_0"), sem("scattered_1")]
        rec_loaded = sem("rec_loaded")
        tables_ready = sem("tables_ready")
        x_loaded = [sem("x_loaded_0"), sem("x_loaded_1")]
        var_ready = sem("var_ready")
        std_ready = sem("std_ready")
        ln_step = sem("ln_step")
        lnT_ready = sem("lnT_ready")
        lnT_copied = sem("lnT_copied")
        ln_rows_ready = sem("ln_rows_ready")
        w_turned = sem("w_turned")
        w_copied = sem("w_copied")
        idx_loaded = [sem(f"idx_loaded_{i}") for i in range(ISETS)]
        pool_turns = sem("pool_turns")
        gathered = [[sem(f"gathered_{a}_{j}") for j in range(GROUP)] for a in range(2)]
        oh_ready = sem("oh_ready")
        sets_done = sem("sets_done")
        agg_done = sem("agg_done")
        s_ready = sem("s_ready")
        gates_done = sem("gates_done")
        rz_ready = sem("rz_ready")
        t_done = sem("t_done")
        t2_ready = sem("t2_ready")
        n_ready = sem("n_ready")
        upd_step = sem("upd_step")
        h_ready = sem("h_ready")
        rows_turned = sem("rows_turned")
        rows_copied = sem("rows_copied")
        rows_stored = sem("rows_stored")
        fin_rows = [sem("fin_rows_0"), sem("fin_rows_1")]
        fin_step = sem("fin_step")
        fin_ready = sem("fin_ready")
        out_stored = sem("out_stored")

        verdict_sb = sb("verdict_sb", [1, 1], I32)
        verdict_loaded = sem("verdict_loaded")

        block = mem.enter_context(nc.Block())

        def x_tiles(t, g, first):
            lo_row = g * LNT * P
            n_full = min(LNT, NFULL - g * LNT)
            pieces = [(t[lo_row:lo_row + n_full * P, :].rearrange("(t p) f -> p t f", p=P), first[:, 0:n_full, :])]
            if n_full < LNT:
                pieces.append((t[NFULL * P:N, :], first[0:NREM, n_full, :]))
            return pieces

        def fin_bufs(b):
            return early[:, b * LNT * P:(b + 1) * LNT * P].bitcast(F16).rearrange("p (t k) -> p t k", k=2 * H)

        PIECES = [len(x_tiles(x, g, xg[:, 0])) for g in range(NLN)]

        def store_ln(sp, g):
            sp.wait_ge(ln_rows_ready, g + 1)
            at = g * LNT * P
            sp.dma_start(hrows[at:at + LNT * P, :].rearrange("(t p) k -> p t k", p=P),
                         lnrow[:].rearrange("p t a k -> p t (a k)")).then_inc(rows_stored, 16)

        def store_out(sp, g):
            sp.wait_ge(fin_ready, g + 1)
            for rows, tile in x_tiles(out, g, xg[:, g % 2]):
                sp.dma_start(rows, tile).then_inc(out_stored, 16)

        @block.sync
        def _(sp):
            sp.dma_start(verdict_sb[:], verdict).then_inc(verdict_loaded, 16)
            sp.wait_ge(verdict_loaded, 16)
            fast = sp.value_load(verdict_sb[0:1, 0:1], min_val=0, max_val=1)
            with sp.If(fast < 1):
                sp.wait_ge(edges_padded, 2)
                for flat, tile in ((src, src_sb), (dst, dst_sb)):
                    sp.dma_start(tile[0:FULL, :], flat[0:FULL * K].rearrange("(p k) -> p k", k=K)).then_inc(edges_loaded, 16)
                    sp.dma_start(tile[FULL:P, 0:REM], flat[FULL * K:E].rearrange("(a k) -> a k", a=1)).then_inc(edges_loaded, 16)
                sp.wait_ge(fill_ready, 1)
                sp.dma_start(rec_dram.rearrange("(p t) o -> p (t o)", p=P), fill[:]).then_inc(rec_filled, 16)
                sp.wait_ge(zeros_ready, 1)
                zeros = hT[:].bitcast(F16)
                sp.dma_start(hrows[NPAD:2 * NPAD, :].rearrange("(p r) k -> p (r k)", p=P), zeros).then_inc(zeros_stored, 16)
                sp.dma_start(hrows[NT * P:NPAD, :].rearrange("(p r) k -> p (r k)", p=P),
                             zeros[:, 0:(NPAD - NT * P) // P * 2 * H]).then_inc(zeros_stored, 16)
                sp.dma_start(wmsg_sb[:], W_msg).then_inc(weights_loaded, 16)
                sp.dma_start(wih_sb[:], W_ih.rearrange("(g p) k -> p g k", p=P)).then_inc(weights_loaded, 16)
                sp.dma_start(whh_sb[:], W_hh.rearrange("(g p) k -> p g k", p=P)).then_inc(weights_loaded, 16)
                sp.dma_start(bmsg_sb[:], b_msg.rearrange("(p o) -> p o", o=1)).then_inc(weights_loaded, 16)
                for g in range(3):
                    sp.dma_start(bih_sb[:, g:g + 1], b_ih[g * P:(g + 1) * P].rearrange("(p o) -> p o", o=1)).then_inc(weights_loaded, 16)
                    sp.dma_start(bhh_sb[:, g:g + 1], b_hh[g * P:(g + 1) * P].rearrange("(p o) -> p o", o=1)).then_inc(weights_loaded, 16)
                for g in range(NLN):
                    if g >= 2:
                        sp.wait_ge(ln_rows_ready, g - 1)
                        sp.wait_ge(lnT_copied, (g - 1) * LNT)
                    for rows, tile in x_tiles(x, g, xg[:, g % 2]):
                        sp.dma_start(tile, rows).then_inc(x_loaded[g % 2], 16)
                    if g >= 1:
                        store_ln(sp, g - 1)
                store_ln(sp, NLN - 1)
                for h in range(2):
                    sp.wait_ge(scattered[h], 16 * SC_HALF * (K // (2 * SC_HALF)))
                sp.dma_start(rec_sb[:], rec_dram.rearrange("(p t) o -> p (t o)", p=P)).then_inc(rec_loaded, 16)
                sp.wait_ge(tables_ready, 1)
                total = sp.value_load(chunk_end[0:1, NCH:NCH + 1], min_val=1, max_val=GMAX)
                with sp.Fori(0, STEPS) as s:
                    with sp.Fori(0, total, ISETS) as g:
                        for i in range(ISETS):
                            n = s * total + g + i + 1
                            for j in range(GROUP):
                                sp.wait_ge(gathered[i % 2][j], ((n + 1 - i % 2) // 2) * 16)
                            sp.dma_start(idx_slot[:, i * GROUP:(i + 1) * GROUP],
                                         idx_tab[:, bass.ds((s % 2) * T + (g + i).with_bounds(max_val=GMAX - 1) * GROUP, GROUP)]
                                         ).then_inc(idx_loaded[i], 16)
                sp.wait_ge(rows_stored, 16 * (NLN + STEPS * NCH))
                par = STEPS % 2
                for g in range(NLN):
                    if g >= 2:
                        sp.wait_ge(fin_ready, g - 1)
                        sp.wait_ge(out_stored, 16 * sum(PIECES[:g - 1]))
                    at = par * NPAD + g * LNT * P
                    sp.dma_start(fin_bufs(g % 2), hrows[at:at + LNT * P, :].rearrange("(t p) k -> p t k", p=P)).then_inc(fin_rows[g % 2], 16)
                    for rows, tile in x_tiles(x, g, xg[:, g % 2]):
                        sp.dma_start(tile, rows).then_inc(fin_rows[g % 2], 16)
                    if g >= 1:
                        store_out(sp, g - 1)
                store_out(sp, NLN - 1)
                sp.wait_ge(out_stored, 16 * sum(PIECES))

        @block.gpsimd
        def _(pool):
            pool.wait_ge(verdict_loaded, 16)
            fast = pool.value_load(verdict_sb[0:1, 0:1], min_val=0, max_val=1)
            with pool.If(fast < 1):
                nc.gpsimd.iota(iota_i[:], pattern=[[1, CHUNK]], base=0, channel_multiplier=0).then_inc(iota_done, 1)
                nc.gpsimd.iota(part_i[:], pattern=[[0, 1]], base=0, channel_multiplier=1).then_inc(iota_done, 1)
                pool.wait_ge(iota_done, 2)
                for turn in range(PRIME):
                    for k in range(2 * GROUP):
                        if turn:
                            pool.wait_ge(gathered[k // GROUP][k % GROUP], 16 * turn)
                        nc.gpsimd.indirect_dma_start(G[:, k * 2 * H:(k + 1) * 2 * H].bitcast(F32), None, x,
                                                     bass.IndirectOffsetOnAxis(ap=part_i[:, 0:1], axis=0)
                                                     ).then_inc(gathered[k // GROUP][k % GROUP], 16)
                pool.wait_ge(rec_filled, 16)
                with pool.Fori(1, K // (2 * SC_HALF) + 1) as i:
                    for h in range(2):
                        pool.wait_ge(slots_filled[h], i)
                        pool.sem_inc(pool_turns, 1)
                        for j in range(h * SC_HALF, (h + 1) * SC_HALF):
                            nc.gpsimd.indirect_dma_start(
                                rec_dram, bass.IndirectOffsetOnAxis(ap=sc_pos[:, j:j + 1], axis=0),
                                sc_rec[:, j:j + 1], None).then_inc(scattered[h], 16)
                pool.wait_ge(rows_stored, 16 * NLN)
                pool.wait_ge(zeros_stored, 32)
                pool.wait_ge(tables_ready, 1)
                total = pool.value_load(chunk_end[0:1, NCH:NCH + 1], min_val=1, max_val=GMAX)
                with pool.Fori(0, STEPS) as s:
                    pool.wait_ge(rows_stored, s * (16 * NCH) + 16 * NLN)
                    first = pool.snap(s * total * 8)
                    with pool.Fori(first + 8 * ISETS, first + total * 8 + 8 * ISETS, 8 * ISETS) as v:
                        for i in range(ISETS):
                            pool.wait_ge(sets_done, (v // 8) + i)
                            pool.wait_ge(idx_loaded[i], v // 2)
                            pool.sem_inc(pool_turns, 1)
                            for j in range(GROUP):
                                k, m = (i % 2) * GROUP + j, i * GROUP + j
                                nc.gpsimd.indirect_dma_start(
                                    G[:, k * 2 * H:(k + 1) * 2 * H], None, hrows,
                                    bass.IndirectOffsetOnAxis(ap=idx_slot[:, m:m + 1], axis=0)).then_inc(gathered[i % 2][j], 16)

        @block.scalar
        def _(act):
            act.wait_ge(verdict_loaded, 16)
            fast = act.value_load(verdict_sb[0:1, 0:1], min_val=0, max_val=1)
            with act.If(fast < 1):
                def fill_half(i, h, wait):
                    if wait is not None:
                        act.wait_ge(scattered[h], wait)
                    col = i * (2 * SC_HALF) + h * SC_HALF
                    lo_c, hi_c = h * SC_HALF, (h + 1) * SC_HALF
                    nc.scalar.copy(sc_pos[:, lo_c:hi_c], pos_i[:, bass.ds(col, SC_HALF)])
                    nc.scalar.copy(sc_rec[:, lo_c:hi_c], rec[:, bass.ds(col, SC_HALF)]).then_inc(slots_filled[h], 1)

                TURNS = K // (2 * SC_HALF)
                act.wait_ge(pos_ready, 1)
                for h in range(2):
                    fill_half(0, h, None)
                cuts = [1] + [TURNS * (g + 1) // (NLN + 2) for g in range(NLN)] + [TURNS]
                for n in range(NLN + 1):
                    with act.Fori(cuts[n], cuts[n + 1]) as i:
                        for h in range(2):
                            fill_half(i, h, i * (16 * SC_HALF))
                    if n < NLN:
                        act.wait_ge(var_ready, n + 1)
                        nc.scalar.activation(std[:], mv[:, :, 1], ACT.Sqrt).then_inc(std_ready, 1)

                def scale_sum(q, first):
                    act.wait_ge(agg_done, q)
                    if first is not None:
                        nc.scalar.copy(deg[0:1, bass.ds(first, CHUNK)], ps_deg[0:1, :])
                    nc.scalar.mul(S, ps_agg[:, bass.ds((q % 2) * CHUNK, CHUNK)], 1.0 / SCALE).then_inc(s_ready, 1)

                def gates(q):
                    act.wait_ge(gates_done, q)
                    act.wait_ge(h_ready, q)
                    nc.scalar.activation(r_sb, ps_r[:], ACT.Sigmoid, bias=bsum[:, 0:1])
                    nc.scalar.activation(z_sb, ps_z[:], ACT.Sigmoid, bias=bsum[:, 1:2]).then_inc(rz_ready, 1)

                def new(q):
                    act.wait_ge(t2_ready, q)
                    nc.scalar.activation(n_sb[:], t_sb[:], ACT.Tanh, bias=bih_sb[:, 2:3]).then_inc(n_ready, 1)

                def rows(q, s, c):
                    act.wait_ge(rows_turned, q + 1)
                    act.wait_ge(rows_stored, q * 16 + (16 * NLN - 16))
                    nc.scalar.copy(rowbuf, ps_rows[:]).then_inc(rows_copied, 1)
                    act.wait_ge(rows_copied, q + 1)
                    at = ((s + 1) % 2) * NPAD + c * CHUNK
                    act.dma_start(hrows[bass.ds(at, CHUNK), :].rearrange("(b p) k -> p b k", p=P),
                                  rowbuf.rearrange("p (b k) -> p b k", k=2 * H)).then_inc(rows_stored, 16)

                act.sem_inc(rows_copied, 1)

                def step(s, first):
                    q0 = s * NCH + 1
                    scale_sum(q0, 0 if first else None)
                    gates(q0)
                    with act.Fori(1, NCH) as c:
                        q = s * NCH + c + 1
                        new(q - 1)
                        scale_sum(q, c * CHUNK if first else None)
                        gates(q)
                        rows(q - 1, s, c - 1)
                    new(s * NCH + NCH)
                    rows(s * NCH + NCH, s, NCH - 1)

                step(0, True)
                with act.Fori(1, STEPS) as s:
                    step(s, False)

        @block.tensor
        def _(pe):
            pe.wait_ge(verdict_loaded, 16)
            fast = pe.value_load(verdict_sb[0:1, 0:1], min_val=0, max_val=1)
            with pe.If(fast < 1):
                pe.sem_inc(sets_done, 5)
                pe.sem_inc(rows_turned, 1)
                pe.wait_ge(counts_ready, 1)
                pe.matmul(ps_r[:, 0:NCH], lhsT=ones_f[:], rhs=cnt[:], start=True, stop=True)
                pe.matmul(ps_z[:, 0:NCH], lhsT=before[:], rhs=cnt[:], start=True, stop=True).then_inc(prefix_ready, 1)
                pe.wait_ge(weights_loaded, 16 * 10)
                for g in range(3):
                    pe.transpose(ps_in[:, g * P:(g + 1) * P], wih_sb[:, g, :], ident[:])
                for g in range(3):
                    mm = pe.transpose(ps_hn[:, g * P:(g + 1) * P], whh_sb[:, g, :], ident[:])
                mm.then_inc(w_turned, 1)
                pe.wait_ge(w_copied, 1)
                pe.matmul(ps_in[:, 0:3 * P], lhsT=wmsg_sb[:], rhs=wihT[:], start=True, stop=True)
                pe.matmul(ps_hn[0:1, 0:3 * P], lhsT=bmsg_sb[:, 0:1], rhs=wihT[:], start=True, stop=True).then_inc(w_turned, 1)
                for g in range(NLN):
                    pe.wait_ge(ln_rows_ready, g + 1)
                    for t in range(LNT):
                        n = g * LNT + t
                        if n >= 2:
                            pe.wait_ge(lnT_copied, n - 1)
                        bank = ps_agg[:, (n % 2) * CHUNK:(n % 2) * CHUNK + P]
                        pe.transpose(bank, xg[:, g % 2, t, :], ident[:]).then_inc(lnT_ready, 1)
                pe.wait_ge(w_copied, 3)
                pe.wait_ge(lnT_copied, NT)
                pe.wait_ge(tables_ready, 1)

                def sums(q, n0, c, first):
                    start = pe.value_load(chunk_end[0:1, bass.ds(c, 1)], min_val=0, max_val=GMAX)
                    end = pe.value_load(chunk_end[0:1, bass.ds(c + 1, 1)], min_val=1, max_val=GMAX)
                    pe.wait_ge(s_ready, q)
                    bank = ps_agg[:, bass.ds((q % 2) * CHUNK, CHUNK)]
                    pe.matmul(bank, lhsT=zeros_h[0:1, 0:P], rhs=zeros_h[:], start=True, stop=False)
                    if first:
                        pe.matmul(ps_deg[0:1, :], lhsT=zeros_h[0:1, 0:1], rhs=zeros_h[:], start=True, stop=False)
                    with pe.Fori(start + n0, end + n0) as n:
                        pe.wait_ge(oh_ready, n)
                        for j in range(GROUP):
                            pe.wait_ge(gathered[0][j], ((n + 1) // 2) * 16 + 16 * PRIME)
                            pe.wait_ge(gathered[1][j], (n // 2) * 16 + 16 * PRIME)
                            g_at = (((n + 1) % 2) * GROUP + j) * (2 * H)
                            hot = OH[:, bass.ds(((n % (OHR // GROUP)) * GROUP + j) * CHUNK, CHUNK)]
                            pe.matmul(bank, lhsT=G[:, bass.ds(g_at, H)], rhs=hot, start=False, stop=False)
                            if first:
                                pe.matmul(ps_deg[0:1, :], lhsT=ones_h[:, 0:1], rhs=hot, start=False, stop=False)
                            mm = pe.matmul(bank, lhsT=G[:, bass.ds(g_at + H, H)], rhs=hot, start=False, stop=False)
                        mm.then_inc(sets_done, 1)
                    if first:
                        pe.matmul(ps_deg[0:1, :], lhsT=zeros_h[0:1, 0:1], rhs=zeros_h[:], start=False, stop=True)
                    pe.matmul(bank, lhsT=zeros_h[0:1, 0:P], rhs=zeros_h[:], start=False, stop=True).then_inc(agg_done, 1)

                def gates(q, c, before=True):
                    pe.wait_ge(s_ready, q + 1)
                    if before:
                        pe.wait_ge(t2_ready, q - 1)
                        pe.wait_ge(rz_ready, q - 1)
                    cols = bass.ds(c * CHUNK, CHUNK)
                    h_c, d_c = hT[:, cols], deg[0:1, cols]
                    for g, bank in ((0, ps_r), (1, ps_z)):
                        w = slice(g * P, (g + 1) * P)
                        pe.matmul(bank[:], lhsT=wfT[:, w], rhs=S, start=True, stop=False)
                        pe.matmul(bank[:], lhsT=whhT[:, w], rhs=h_c, start=False, stop=False)
                        pe.matmul(bank[:], lhsT=cdeg[0:1, w], rhs=d_c, start=False, stop=True)
                    w = slice(2 * P, 3 * P)
                    pe.matmul(ps_hn[:], lhsT=whhT[:, w], rhs=h_c, start=True, stop=True)
                    pe.matmul(ps_in[:], lhsT=wfT[:, w], rhs=S, start=True, stop=False)
                    pe.matmul(ps_in[:], lhsT=cdeg[0:1, w], rhs=d_c, start=False, stop=True).then_inc(gates_done, 1)

                def turn(q):
                    pe.wait_ge(h_ready, q + 1)
                    pe.wait_ge(rows_copied, q)
                    for b in range(4):
                        for a, part in enumerate((hi, lo)):
                            mm = pe.transpose(ps_rows[:, (2 * b + a) * P:(2 * b + a + 1) * P], part[:, b * P:(b + 1) * P], ident_h[:])
                    mm.then_inc(rows_turned, 1)

                pe.sem_inc(s_ready, 1)
                total = pe.value_load(chunk_end[0:1, NCH:NCH + 1], min_val=1, max_val=GMAX)

                def step(s, first):
                    n0 = pe.snap(s * total + 1) if not first else 1
                    q0 = s * NCH + 1
                    sums(q0, n0, 0, first)
                    gates(q0, 0, before=not first)
                    with pe.Fori(1, NCH) as c:
                        q = s * NCH + c + 1
                        sums(q, n0, c, first)
                        gates(q, c)
                        turn(q - 1)
                    turn(s * NCH + NCH)

                step(0, True)
                with pe.Fori(1, STEPS) as s:
                    step(s, False)

        @block.vector
        def _(dve):
            dve.wait_ge(verdict_loaded, 16)
            fast = dve.value_load(verdict_sb[0:1, 0:1], min_val=0, max_val=1)
            with dve.If(fast < 1):
                done = [0]

                def link(ins):
                    done[0] += 1
                    ins.then_inc(dve_step, 1)
                    dve.wait_ge(dve_step, done[0])

                nc.vector.memset(src_sb[96:P, REM:K], NPAD - 1).then_inc(edges_padded, 1)
                nc.vector.memset(dst_sb[96:P, REM:K], 0).then_inc(edges_padded, 1)
                nc.vector.memset(fill[:], NO_NODE).then_inc(fill_ready, 1)
                dve.sem_inc(h_ready, 1)
                nc.vector.memset(ones_f[:], 1.0)
                nc.vector.memset(ones_h[:], 1.0)
                nc.vector.memset(zeros_h[:], 0.0)
                nc.vector.memset(hT[:], 0.0).then_inc(zeros_ready, 1)
                dve.wait_ge(iota_done, 2)
                nc.vector.tensor_copy(iota_h[:], iota_i[:])
                nc.vector.tensor_copy(iota_f[:], iota_i[:, 0:P])
                link(nc.vector.tensor_copy(part_f[:], part_i[:]))
                nc.vector.tensor_scalar(ident[:], iota_f[:], part_f[:, 0:1], None, ALU.is_equal)
                nc.vector.tensor_scalar(ident_h[:], iota_f[:], part_f[:, 0:1], None, ALU.is_equal)
                link(nc.vector.tensor_scalar(before[:], iota_f[:], part_f[:, 0:1], None, ALU.is_gt))
                nc.vector.memset(pos, 0.0).then_inc(pos_cleared, 1)
                dve.wait_ge(edges_loaded, 64)
                link(nc.vector.tensor_scalar(chunk_i, src_sb, 9, None, ALU.logical_shift_right))
                link(nc.vector.tensor_copy(chunk_b[:], chunk_i))
                link(nc.vector.tensor_scalar(chunk_i, src_sb, CHUNK - 1, None, ALU.bitwise_and))
                link(nc.vector.scalar_tensor_tensor(out=rec, in0=dst_sb, scalar=10, in1=chunk_i,
                                                    op0=ALU.logical_shift_left, op1=ALU.bitwise_or))
                with dve.Fori(0, NCH) as b:
                    nc.vector.tensor_scalar(mask[:], chunk_b[:], iota_f[:, bass.ds(b, 1)], None, ALU.is_equal).then_inc(mask_step, 1)
                    dve.wait_ge(mask_step, b + 1)
                    nc.vector.tensor_reduce(cnt[:, bass.ds(b, 1)], mask[:], AX_X, ALU.add).then_inc(rank_step, 1)
                    dve.wait_ge(rank_step, b + 1)
                dve.drain().then_inc(counts_ready, 1)
                dve.wait_ge(prefix_ready, 1)
                link(nc.vector.tensor_scalar(grp_f[:], ps_r[:, 0:NCH], float(GE - 1), float(GE), ALU.add, ALU.max))
                link(nc.vector.tensor_copy(grp_i[:], grp_f[:]))
                shift = GE.bit_length() - 1
                link(nc.vector.tensor_scalar(grp_i[:], grp_i[:], shift, None, ALU.logical_shift_right))
                link(nc.vector.tensor_copy(grp_f[:], grp_i[:]))
                link(nc.vector.tensor_copy(cum[:, 0, :], grp_i[:]))
                a, d = 0, 1
                while d < NCH:
                    nc.vector.tensor_copy(cum[:, 1 - a, 0:d], cum[:, a, 0:d])
                    link(nc.vector.tensor_tensor(cum[:, 1 - a, d:NCH], cum[:, a, d:NCH], cum[:, a, 0:NCH - d], ALU.add))
                    a, d = 1 - a, 2 * d
                link(nc.vector.tensor_tensor(start_f[:], cum[:, a, :], grp_f[:], ALU.subtract))
                nc.vector.tensor_copy(chunk_end[:, 0:NCH], start_f[:])
                link(nc.vector.tensor_scalar(chunk_end[:, NCH:NCH + 1], cum[:, a, NCH - 1:NCH], float(ISETS - 1), None, ALU.add))
                link(nc.vector.tensor_scalar(chunk_end[:, NCH:NCH + 1], chunk_end[:, NCH:NCH + 1], 0x7FFFFFFF - (ISETS - 1), None, ALU.bitwise_and))
                link(nc.vector.tensor_scalar(base[:], start_f[:], float(GE), None, ALU.mult))
                link(nc.vector.tensor_tensor(base[:], base[:], ps_z[:, 0:NCH], ALU.add))
                with dve.Fori(1, NCH + 1) as b:
                    nc.vector.tensor_scalar(mask[:], chunk_b[:], iota_f[:, bass.ds(b - 1, 1)], None, ALU.is_equal).then_inc(chunk_masked, 1)
                    dve.wait_ge(chunk_masked, b)
                    nc.vector.tensor_tensor_scan(scan, mask[:], mask[:], base[:, bass.ds(b - 1, 1)], ALU.add, ALU.max).then_inc(chunk_ranked, 1)
                    dve.wait_ge(pos_cleared, 1)
                    dve.wait_ge(chunk_ranked, b)
                    nc.vector.copy_predicated(pos, mask[:], scan).then_inc(chunk_placed, 1)
                    dve.wait_ge(chunk_placed, b)
                link(nc.vector.tensor_scalar(pos_i, pos, -1.0, None, ALU.add))
                link(nc.vector.tensor_scalar(pos_hi, pos_i, 7, None, ALU.logical_shift_right))
                link(nc.vector.tensor_scalar(pos_i, pos_i, P - 1, None, ALU.bitwise_and))
                link(nc.vector.scalar_tensor_tensor(out=pos, in0=pos_i, scalar=float(T), in1=pos_hi, op0=ALU.mult, op1=ALU.add))
                nc.vector.tensor_copy(pos_i, pos).then_inc(pos_ready, 1)
                dve.wait_ge(w_turned, 1)
                nc.vector.tensor_copy(wihT[:], ps_in[:, 0:3 * P])
                nc.vector.tensor_copy(whhT[:], ps_hn[:, 0:3 * P]).then_inc(w_copied, 1)
                dve.wait_ge(w_turned, 2)
                nc.vector.tensor_copy(wfT[:], ps_in[:, 0:3 * P])
                nc.vector.tensor_copy(cdeg[:], ps_hn[0:1, 0:3 * P]).then_inc(w_copied, 1)
                nc.vector.tensor_tensor(bsum[:], bih_sb[:], bhh_sb[:], ALU.add).then_inc(w_copied, 1)
                loaded = [0, 0]
                for g in range(NLN):
                    loaded[g % 2] += 16 * PIECES[g]
                    xt = xg[:, g % 2]
                    dve.wait_ge(x_loaded[g % 2], loaded[g % 2])
                    for t in range(LNT):
                        link(nc.vector.bn_stats(stats[:], xt[:, t, :]))
                        link(nc.vector.bn_aggr(mv[:, t, :], stats[:]))
                    link(nc.vector.tensor_scalar(mv[:, :, 1], mv[:, :, 1], EPS, None, ALU.add))
                    dve.sem_inc(var_ready, 1)
                    dve.wait_ge(std_ready, g + 1)
                    link(nc.vector.reciprocal(rstd[:], std[:]))
                    for t in range(LNT):
                        last = nc.vector.tensor_scalar(xt[:, t, :], xt[:, t, :], mv[:, t, 0:1], rstd[:, t:t + 1], ALU.subtract, ALU.mult)
                    link(last)
                    link(nc.vector.tensor_scalar(xt, xt, 0.0, None, ALU.max))
                    if g >= 1:
                        dve.wait_ge(rows_stored, 16 * g)
                    link(nc.vector.tensor_scalar(lnrow[:, :, 0, :], xt, SCALE, None, ALU.mult))
                    nc.vector.scalar_tensor_tensor(out=lnrow[:, :, 1, :], in0=xt, scalar=SCALE, in1=lnrow[:, :, 0, :],
                                                   op0=ALU.mult, op1=ALU.subtract).then_inc(ln_rows_ready, 1)
                    dve.wait_ge(zeros_stored, 32)
                    for t in range(LNT):
                        n = g * LNT + t
                        dve.wait_ge(lnT_ready, n + 1)
                        nc.vector.tensor_copy(hT[:, n * P:(n + 1) * P],
                                              ps_agg[:, (n % 2) * CHUNK:(n % 2) * CHUNK + P]).then_inc(lnT_copied, 1)
                dve.wait_ge(rec_loaded, 16)
                nc.vector.tensor_scalar(idx_tab[:, 0:T], rec_sb[:], 10, None, ALU.logical_shift_right)
                link(nc.vector.tensor_scalar(rec_sb[:], rec_sb[:], NO_NODE, None, ALU.bitwise_and))
                nc.vector.tensor_copy(loc_tab, rec_sb[:])
                link(nc.vector.tensor_scalar(idx_tab[:, T:2 * T], idx_tab[:, 0:T], float(NPAD), None, ALU.add))
                dve.drain().then_inc(tables_ready, 1)
                total = dve.value_load(chunk_end[0:1, NCH:NCH + 1], min_val=1, max_val=GMAX)

                def hots(n0, c):
                    start = dve.value_load(chunk_end[0:1, bass.ds(c, 1)], min_val=0, max_val=GMAX)
                    end = dve.value_load(chunk_end[0:1, bass.ds(c + 1, 1)], min_val=1, max_val=GMAX)
                    with dve.Fori(start, end) as g:
                        n = dve.snap(g + n0)
                        dve.wait_ge(sets_done, n + 1)
                        for j in range(GROUP):
                            hot = OH[:, bass.ds(((n % (OHR // GROUP)) * GROUP + j) * CHUNK, CHUNK)]
                            ins = nc.vector.tensor_scalar(hot, iota_h[:], loc_tab[:, bass.ds(g * GROUP + j, 1)], None, ALU.is_equal)
                        ins.then_inc(oh_ready, 1)

                def update(q, c):
                    h_c = hT[:, bass.ds(c * CHUNK, CHUNK)]
                    dve.wait_ge(rz_ready, q)
                    nc.vector.scalar_tensor_tensor(out=t_sb[:], in0=ps_hn[:], scalar=bhh_sb[:, 2:3], in1=r_sb,
                                                   op0=ALU.add, op1=ALU.mult).then_inc(t_done, 1)
                    dve.wait_ge(t_done, q)
                    nc.vector.tensor_tensor(t_sb[:], ps_in[:], t_sb[:], ALU.add).then_inc(t2_ready, 1)
                    dve.wait_ge(n_ready, q)
                    nc.vector.tensor_tensor(t_sb[:], h_c, n_sb[:], ALU.subtract).then_inc(upd_step, 1)
                    dve.wait_ge(upd_step, q * 4 - 3)
                    nc.vector.tensor_tensor(t_sb[:], t_sb[:], z_sb, ALU.mult).then_inc(upd_step, 1)
                    dve.wait_ge(upd_step, q * 4 - 2)
                    nc.vector.tensor_tensor(h_c, n_sb[:], t_sb[:], ALU.add).then_inc(upd_step, 1)
                    dve.wait_ge(upd_step, q * 4 - 1)
                    dve.wait_ge(rows_turned, q)
                    nc.vector.tensor_scalar(hi[:], h_c, SCALE, None, ALU.mult).then_inc(upd_step, 1)
                    dve.wait_ge(upd_step, q * 4)
                    nc.vector.scalar_tensor_tensor(out=lo[:], in0=h_c, scalar=SCALE, in1=hi[:],
                                                   op0=ALU.mult, op1=ALU.subtract).then_inc(h_ready, 1)

                with dve.Fori(0, STEPS) as s:
                    n0 = dve.snap(s * total + 1)
                    hots(n0, 0)
                    with dve.Fori(1, NCH) as c:
                        hots(n0, c)
                        update(s * NCH + c, c - 1)
                    update(s * NCH + NCH, NCH - 1)
                loaded = [0, 0]
                for g in range(NLN):
                    loaded[g % 2] += 16 * (1 + PIECES[g])
                    dve.wait_ge(fin_rows[g % 2], loaded[g % 2])
                    rows, xt = fin_bufs(g % 2), xg[:, g % 2]
                    for part in range(2):
                        ins = nc.vector.scalar_tensor_tensor(out=xt, in0=rows[:, :, part * H:(part + 1) * H], scalar=1.0 / SCALE,
                                                             in1=xt, op0=ALU.mult, op1=ALU.add)
                        if part == 0:
                            link(ins)
                    ins.then_inc(fin_ready, 1)


def build_gnn(nc, *args):
    verdict = nc.dram_tensor("verdict", (1, 1), I32, kind="Internal").ap()
    with ExitStack() as ctx:
        steps_only = build_fast(nc, ctx, verdict, *args)
        build_general(nc, ctx, steps_only, verdict, *args)


_INS = ["x", "src", "dst", "L0_gnn_W_msg", "L0_gnn_b_msg", "L0_gnn_W_ih", "L0_gnn_W_hh", "L0_gnn_b_ih", "L0_gnn_b_hh"]


def kernel(**inputs):
    import numpy as _np
    import concourse.bacc as _bacc
    from concourse import mybir as _mybir
    from concourse.bass_utils import run_bass_kernel_spmd as _run

    nc = _bacc.Bacc("TRN2", target_bir_lowering=False, num_devices=1)
    arrays, args = {}, []
    for name in _INS:
        a = _np.ascontiguousarray(inputs[name])
        arrays[f"in_{name}_dram"] = a
        args.append(nc.dram_tensor(f"in_{name}_dram", a.shape, _mybir.dt.from_np(a.dtype), kind="ExternalInput").ap())
    shape = inputs["x"].shape
    args.append(nc.dram_tensor("out_0_dram", shape, _mybir.dt.float32, kind="ExternalOutput").ap())
    build_gnn(nc, *args)
    r = _run(nc, [arrays], core_ids=[0])
    return r.results[0]["out_0_dram"]
```
